# Optimizing a Trainium2 kernel written in Bass

```python
import numpy as np
import jax
import jax.numpy as jnp

def _softmax(x, axis=-1):
    return jax.nn.softmax(x, axis=axis)

def _gelu(x):
    return jax.nn.gelu(x, approximate=True)

def _silu(x):
    return jax.nn.silu(x)

def _sigmoid(x):
    return jax.nn.sigmoid(x)

def _layernorm(x, axis=-1, eps=1e-05):
    m = jnp.mean(x, axis=axis, keepdims=True)
    v = jnp.var(x, axis=axis, keepdims=True)
    return (x - m) / jnp.sqrt(v + eps)

def _scatter_add(tgt, idx, src, axis=0):
    return tgt.at[idx].add(src)

def _segment_sum(src, seg, n):
    return jax.ops.segment_sum(src, seg, n)
kernel_name = 'mk_adj_resnorm_d2_adj_r2_71ba31'

def setup_inputs(seed: int=0):
    np.random.seed(seed)
    _w = jnp.asarray

    def _rec_inputs():
        import jax
        import jax.numpy as jnp
        _gk = jax.random.key(seed)
        x = -0.000125 + 0.9999 * jax.random.normal(jax.random.fold_in(_gk, 1), (128, 128, 128), jnp.float32)
        _w = (1.0 + jnp.arange(128, dtype=jnp.float32)) ** (-0.5)
        _w = _w / _w.mean()
        _pij = jnp.clip(0.0625 * _w[:, None] * _w[None, :], 0.0, 1.0)
        _a = jax.random.uniform(jax.random.fold_in(_gk, 2), (128, 128)) < _pij
        _a = jnp.logical_or(_a, jnp.swapaxes(_a, -1, -2))
        _a = jnp.logical_or(_a, jnp.eye(128, dtype=bool))
        _af = _a.astype(jnp.float32)
        _af = _af * jax.random.uniform(jax.random.fold_in(_gk, 3), (128, 128), jnp.float32, 0.05, 0.000488281)
        adj = _af
        return (x, adj)
    x, adj = _rec_inputs()

    def _L0_gnn_setup():
        import jax, jax.numpy as jnp
        import numpy as np
        B, T, D, H = (64, 1024, 128, 128)
        MAX_SKIP = 4

        def _lstm_last(Wih, Whh, bih, bhh, xs):
            N, _, Hd = xs.shape
            bias = bih + bhh

            def step(carry, x_t):
                h, c = carry
                g = x_t @ Wih.T + h @ Whh.T + bias
                i, f, gg, o = jnp.split(g, 4, axis=-1)
                c = jax.nn.sigmoid(f) * c + jax.nn.sigmoid(i) * jnp.tanh(gg)
                h = jax.nn.sigmoid(o) * jnp.tanh(c)
                return ((h, c), None)
            init = (jnp.zeros((N, Hd), xs.dtype), jnp.zeros((N, Hd), xs.dtype))
            (h_last, _), _ = jax.lax.scan(step, init, jnp.swapaxes(xs, 0, 1))
            return h_last
        key = jax.random.key(seed)
        ks = jax.random.split(key, 8)
        s = 0.05
        x = jax.random.normal(ks[0], (B, T, D), jnp.float32)
        adj = jax.random.uniform(ks[1], (T, T), jnp.float32) / T
        Wg0 = jax.random.normal(ks[2], (D, H), jnp.float32) * s
        bg0 = jnp.zeros((H,), jnp.float32)
        Wg1 = jax.random.normal(ks[3], (H, H), jnp.float32) * s
        bg1 = jnp.zeros((H,), jnp.float32)
        Wih = jax.random.normal(ks[4], (MAX_SKIP, 4 * H, H), jnp.float32) * s
        Whh = jax.random.normal(ks[5], (MAX_SKIP, 4 * H, H), jnp.float32) * s
        bih = jax.random.normal(ks[6], (MAX_SKIP, 4 * H), jnp.float32) * s
        bhh = jax.random.normal(ks[7], (MAX_SKIP, 4 * H), jnp.float32) * s
        return dict(x=x, adj=adj, Wg0=Wg0, bg0=bg0, Wg1=Wg1, bg1=bg1, Wih=Wih, Whh=Whh, bih=bih, bhh=bhh)
    _L0_gnn_all = _L0_gnn_setup()
    _L0_gnn_in = {k: v for k, v in _L0_gnn_all.items() if k in ('Wg0', 'bg0', 'Wg1', 'bg1', 'Wih', 'Whh', 'bih', 'bhh')}
    del _L0_gnn_all

    def _L1_gnn_setup():
        import jax, jax.numpy as jnp
        import numpy as np
        BT, N, D, HEADS, E = (512, 64, 128, 4, 256)
        LRELU_SLOPE = 0.2
        EPS = 1e-08
        key = jax.random.key(seed)
        ks = jax.random.split(key, 8)
        d = D
        return {'H': jax.random.normal(ks[0], (BT, N, d), jnp.float32), 'W_lin': jax.random.normal(ks[1], (d, d), jnp.float32) / np.sqrt(d).astype(np.float32), 'W_val': jax.random.normal(ks[2], (d, d), jnp.float32) / np.sqrt(d).astype(np.float32), 'a': jax.random.normal(ks[3], (HEADS, d // HEADS), jnp.float32), 'W_out': jax.random.normal(ks[4], (d, d), jnp.float32) / np.sqrt(d).astype(np.float32), 'A0': jax.random.uniform(ks[5], (N, N), jnp.float32), 'src': jax.random.randint(ks[6], (E,), 0, N, jnp.int32), 'dst': jax.random.randint(ks[7], (E,), 0, N, jnp.int32)}
    _L1_gnn_all = _L1_gnn_setup()
    _L1_gnn_in = {k: v for k, v in _L1_gnn_all.items() if k in ('W_lin', 'W_val', 'a', 'W_out', 'src', 'dst')}
    del _L1_gnn_all
    return {'x': x, 'adj': adj, 'L0_gnn_Wg0': _L0_gnn_in['Wg0'], 'L0_gnn_bg0': _L0_gnn_in['bg0'], 'L0_gnn_Wg1': _L0_gnn_in['Wg1'], 'L0_gnn_bg1': _L0_gnn_in['bg1'], 'L0_gnn_Wih': _L0_gnn_in['Wih'], 'L0_gnn_Whh': _L0_gnn_in['Whh'], 'L0_gnn_bih': _L0_gnn_in['bih'], 'L0_gnn_bhh': _L0_gnn_in['bhh'], 'L1_gnn_W_lin': _L1_gnn_in['W_lin'], 'L1_gnn_W_val': _L1_gnn_in['W_val'], 'L1_gnn_a': _L1_gnn_in['a'], 'L1_gnn_W_out': _L1_gnn_in['W_out'], 'L1_gnn_src': _L1_gnn_in['src'], 'L1_gnn_dst': _L1_gnn_in['dst']}

def reference(x, adj, L0_gnn_Wg0, L0_gnn_bg0, L0_gnn_Wg1, L0_gnn_bg1, L0_gnn_Wih, L0_gnn_Whh, L0_gnn_bih, L0_gnn_bhh, L1_gnn_W_lin, L1_gnn_W_val, L1_gnn_a, L1_gnn_W_out, L1_gnn_src, L1_gnn_dst):
    import jax
    import jax.numpy as jnp

    def _L0_gnn_ref(x, adj, Wg0, bg0, Wg1, bg1, Wih, Whh, bih, bhh):
        import jax, jax.numpy as jnp
        import numpy as np
        B, T, D, H = (64, 1024, 128, 128)
        MAX_SKIP = 4

        def _lstm_last(Wih, Whh, bih, bhh, xs):
            N, _, Hd = xs.shape
            bias = bih + bhh

            def step(carry, x_t):
                h, c = carry
                g = x_t @ Wih.T + h @ Whh.T + bias
                i, f, gg, o = jnp.split(g, 4, axis=-1)
                c = jax.nn.sigmoid(f) * c + jax.nn.sigmoid(i) * jnp.tanh(gg)
                h = jax.nn.sigmoid(o) * jnp.tanh(c)
                return ((h, c), None)
            init = (jnp.zeros((N, Hd), xs.dtype), jnp.zeros((N, Hd), xs.dtype))
            (h_last, _), _ = jax.lax.scan(step, init, jnp.swapaxes(xs, 0, 1))
            return h_last
        h = jax.nn.relu(jnp.einsum('ts,bsh->bth', adj, x @ Wg0 + bg0))
        h = jax.nn.relu(jnp.einsum('ts,bsh->bth', adj, h @ Wg1 + bg1))
        Bv, Tv, Hd = h.shape
        for p in range(1, MAX_SKIP + 1):
            nw = Tv // p
            wins = h[:, :nw * p, :].reshape(Bv * nw, p, Hd)
            last = _lstm_last(Wih[p - 1], Whh[p - 1], bih[p - 1], bhh[p - 1], wins)
            idx = jnp.arange(nw) * p + (p - 1)
            h = h.at[:, idx, :].set(last.reshape(Bv, nw, Hd))
        return h

    def _L1_gnn_ref(H, W_lin, W_val, a, W_out, A0, src, dst):
        import jax, jax.numpy as jnp
        import numpy as np
        BT, N, D, HEADS, E = (512, 64, 128, 4, 256)
        LRELU_SLOPE = 0.2
        EPS = 1e-08
        bt, n, d = H.shape
        h, dh = a.shape
        Xq = (H @ W_lin.T).reshape(bt, n, h, dh)
        Xv = (H @ W_val.T).reshape(bt, n, h, dh)
        Qs = Xq[:, src]
        Kt = Xq[:, dst]
        e = jnp.einsum('behd,hd->beh', jax.nn.leaky_relu(Qs + Kt, LRELU_SLOPE), a)
        e = e + jnp.log(A0[src, dst] + EPS)[None, :, None]
        e_t = e.transpose(1, 0, 2)
        m = jax.ops.segment_max(e_t, src, num_segments=n)
        ex = jnp.exp(e_t - m[src])
        denom = jax.ops.segment_sum(ex, src, num_segments=n)
        attn = ex / denom[src]
        Vt = Xv[:, dst].transpose(1, 0, 2, 3)
        Y = jax.ops.segment_sum(attn[..., None] * Vt, src, num_segments=n)
        Y = Y.transpose(1, 0, 2, 3).reshape(bt, n, d)
        return Y @ W_out.T
    x = _layernorm(x + _L0_gnn_ref(x, adj, L0_gnn_Wg0, L0_gnn_bg0, L0_gnn_Wg1, L0_gnn_bg1, L0_gnn_Wih, L0_gnn_Whh, L0_gnn_bih, L0_gnn_bhh), axis=-1)
    x = _layernorm(x + _L1_gnn_ref(x, L1_gnn_W_lin, L1_gnn_W_val, L1_gnn_a, L1_gnn_W_out, adj, L1_gnn_src, L1_gnn_dst), axis=-1)
    return x

_drawn_inputs = setup_inputs


def setup_inputs(seed=0):
    import zlib

    import numpy as np

    out = dict(_drawn_inputs(seed))
    spreads = {'L0_gnn_bg0': (0.0, 0.8), 'L0_gnn_bg1': (0.0, 0.8)}
    factors = {'L0_gnn_Wg0': 8.0, 'L0_gnn_Wg1': 8.0, 'L0_gnn_Wih': 6.443, 'L0_gnn_Whh': 8.0}
    for name, (base, spread) in spreads.items():
        noise = np.random.default_rng([zlib.crc32(name.encode()), seed]).standard_normal(out[name].shape)
        drawn = base * np.exp(spread * noise) if base else spread * noise
        out[name] = jnp.asarray(drawn.astype(out[name].dtype))
    for name, factor in factors.items():
        out[name] = (out[name] * factor).astype(out[name].dtype)
    return out
```

```python
from contextlib import ExitStack

import concourse.bass as bass
from concourse import mybir
from concourse.alu_op_type import AluOpType as ALU

F32 = mybir.dt.float32
F32R = mybir.dt.float32r
I32 = mybir.dt.int32
ACT = mybir.ActivationFunctionType
AX = mybir.AxisListType

P = 128
BANK = 512
SKIPS = 4
GATES = 4
I, F, G, O = range(GATES)
LN_EPS = 1e-5
LOG_EPS = 1e-8
SLOPE = 0.2
FLT_MAX = 3.4028234e38

BT = 4
GNN_SLOTS = 4


def loop(engine, first, end):
    return engine.bass.Fori(first, end, engines=(engine.engine,), hint_back_edge=True)


class LstmPhase:

    def __init__(self, p, batches, pairs, n_batch, items_before, f_before):
        self.p, self.batches, self.pairs = p, batches, pairs
        self.windows = P // p
        self.width = batches * self.windows
        self.iters = n_batch // (batches * 2 * pairs)
        self.per_iter = 2 * p * pairs
        self.f_per_iter = 2 * (p - 1) * pairs
        self.items_before, self.f_before = items_before, f_before
        self.items_after = items_before + self.iters * self.per_iter
        self.f_after = f_before + self.iters * self.f_per_iter

    def body(self):
        forgets = 0
        for pair in range(self.pairs):
            for t in range(self.p):
                for s in range(2):
                    forgets += t > 0
                    yield 2 * pair + s, t, 2 * (pair * self.p + t) + s, forgets

    def items_for(self, batches):
        tile = -(-batches // self.batches) - 1
        return self.items_before + 2 * self.p * (tile // 2) + 2 * (self.p - 1) + tile % 2 + 1


def lstm_phases(n_batch):
    phases, items, forgets = [], 0, 0
    for p, batches, pairs in ((1, 4, 4), (2, 8, 2), (3, 8, 2), (4, 16, 2)):
        phases.append(LstmPhase(p, batches, pairs, n_batch, items, forgets))
        items, forgets = phases[-1].items_after, phases[-1].f_after
    return phases


def front(nc, hT_hi, hT_lo, ident, adj_sb, psum, x, adj, Wg0, bg0, Wg1, bg1, Wih, Whh, bih, bhh):
    B = x.shape[0]
    tiles = B // BT
    gnn_iters = tiles // GNN_SLOTS
    phases = lstm_phases(B)
    TW = BT * P

    with ExitStack() as ctx:
        def sb(name, shape, dt=F32):
            return ctx.enter_context(nc.sbuf_tensor(name, shape, dt))

        def sem(name):
            return ctx.enter_context(nc.semaphore(name))

        adjT = sb("adjT", [P, P])
        wg0 = sb("wg0", [P, P])
        wg1 = sb("wg1", [P, P])
        ones = sb("ones", [P, 1])
        start = sb("start", [P, 4])
        deg_row = sb("deg_row", [1, BT, P])
        bg0_row = sb("bg0_row", [1, BT, P])
        bg1_row = sb("bg1_row", [1, P])
        w_hi = sb("w_hi", [P, SKIPS, 2, GATES, P], F32R)
        w_lo = sb("w_lo", [P, SKIPS, 2, GATES, P], F32R)
        b_raw = sb("b_raw", [SKIPS * GATES, 2, P])
        b_sum = sb("b_sum", [SKIPS * GATES, P])
        bias = sb("bias", [P, SKIPS * GATES])

        work = sb("work", [P, 15, BANK])
        axT = [work[:, s, :] for s in range(GNN_SLOTS)]
        h1 = [work[:, 4 + s, :].rearrange("p (b h) -> p b h", b=BT) for s in range(GNN_SLOTS)]
        ahT = axT
        x_tile = [work[:, 8 + s, :].rearrange("p (b d) -> p b d", b=BT) for s in range(GNN_SLOTS)]
        w_raw = work[:, 0:4, :].rearrange("p (r j) (g d) -> p r j g d", r=2, g=GATES)
        gate = [[work[:, 4 * s + g, :] for g in range(GATES)] for s in range(2)]
        cell = [work[:, 8 + s, :] for s in range(2)]
        in_gate = work[:, 10, :]
        tanh_c = [work[:, 11 + s, :] for s in range(2)]
        h_full = [work[:, 13 + s, :] for s in range(2)]
        hs_hi = sb("hs_hi", [P, 2, BANK], F32R)
        hs_lo = sb("hs_lo", [P, 2, BANK], F32R)

        ident_zero, ident_ready = sem("ident_zero"), sem("ident_ready")
        ones_ready = sem("ones_ready")
        adj_loaded, gnn_w_loaded, b_loaded = sem("adj_loaded"), sem("gnn_w_loaded"), sem("b_loaded")
        w_loaded = [sem(f"w_loaded{i}") for i in range(2)]
        x_loaded = [sem(f"x_loaded{s}") for s in range(GNN_SLOTS)]
        adjT_psum, adjT_ready, deg_psum, deg_ready = (sem(n) for n in ("adjT_psum", "adjT_ready", "deg_psum", "deg_ready"))
        b_summed, b_psum, b_ready = sem("b_summed"), sem("b_psum"), sem("b_ready")
        w_psum, w_hi_ready, w_lo_ready = sem("w_psum"), sem("w_hi_ready"), sem("w_lo_ready")
        ax_psum, axT_ready = sem("ax_psum"), sem("axT_ready")
        h1_psum, h1_ready = sem("h1_psum"), sem("h1_ready")
        ah_psum, ahT_ready = sem("ah_psum"), sem("ahT_ready")
        h2_psum, h2_hi, h2_done = sem("h2_psum"), sem("h2_hi"), sem("h2_done")
        gate_psum = [sem(f"gate_psum_{n}") for n in "ifgo"]
        gates_read = sem("gates_read")
        f_ready, ig_ready, tanh_ready = sem("f_ready"), sem("ig_ready"), sem("tanh_ready")
        fc_done, ig_done, c_ready = sem("fc_done"), sem("ig_done"), sem("c_ready")
        h_mul, h_hi, h_done = sem("h_mul"), sem("h_hi"), sem("h_done")
        CREDIT = 2

        hi_bt = hT_hi[:, :].rearrange("p (b t) -> p b t", t=P)
        lo_bt = hT_lo[:, :].rearrange("p (b t) -> p b t", t=P)

        def windows_at(ph, view, it, tile, t):
            first = (it * (2 * ph.pairs) + tile) * ph.batches
            return view[:, bass.ds(first, ph.batches), t:t + (ph.windows - 1) * ph.p + 1:ph.p]

        def as_windows(ph, flat):
            return flat.rearrange("p (b w) -> p b w", b=ph.batches)

        block = ctx.enter_context(nc.Block())

        @block.sync
        def _(sp):
            sp.dma_start(adj_sb[:, :], adj).then_inc(adj_loaded, 16)
            sp.dma_start(wg0[:, :], Wg0).then_inc(gnn_w_loaded, 16)
            sp.dma_start(wg1[:, :], Wg1).then_inc(gnn_w_loaded, 16)
            for b in range(BT):
                sp.dma_start(bg0_row[:, b, :], bg0.rearrange("(a h) -> a h", a=1)).then_inc(gnn_w_loaded, 16)
            sp.dma_start(bg1_row[:, :], bg1.rearrange("(a h) -> a h", a=1)).then_inc(gnn_w_loaded, 16)
            sp.dma_start(b_raw[:, 0, :], bih.rearrange("s (g h) -> (s g) h", g=GATES)).then_inc(b_loaded, 16)
            sp.dma_start(b_raw[:, 1, :], bhh.rearrange("s (g h) -> (s g) h", g=GATES)).then_inc(b_loaded, 16)
            for s in range(GNN_SLOTS):
                sp.dma_start(x_tile[s], x[s * BT:(s + 1) * BT].rearrange("b t d -> t b d")).then_inc(x_loaded[s], 16)
            with loop(sp, 0, gnn_iters - 1) as it:
                for s in range(GNN_SLOTS):
                    sp.wait_ge(ax_psum, it * GNN_SLOTS + s + 1)
                    src = x[bass.ds((it * GNN_SLOTS + GNN_SLOTS + s) * BT, BT)]
                    sp.dma_start(x_tile[s], src.rearrange("b t d -> t b d")).then_inc(x_loaded[s], 16)

        @block.gpsimd
        def _(pool):
            pool.memset(ident[:, :], 0.0).then_inc(ident_zero, 1)
            pool.wait_ge(ident_zero, 1)
            pool.affine_select(out=ident[:, :], in_=ident[:, :], compare_op=ALU.not_equal, fill=1.0, base=0,
                               pattern=[[-1, P]], channel_multiplier=1).then_inc(ident_ready, 1)
            for p in range(SKIPS):
                if p >= 2:
                    pool.wait_ge(w_psum, 2 * (p - 1))
                for j, w in enumerate((Wih, Whh)):
                    pool.dma_start(w_raw[:, p % 2, j], w[p].rearrange("(g h) d -> h g d", g=GATES)).then_inc(w_loaded[p % 2], 16)

        @block.tensor
        def _(pe):
            pe.wait_ge(adj_loaded, 16)
            pe.wait_ge(ident_ready, 1)
            pe.transpose(psum[:, 0, 0:P], adj_sb[:, :], ident[:, :]).then_inc(adjT_psum, 1)
            pe.wait_ge(adjT_ready, 1)
            pe.wait_ge(ones_ready, 1)
            pe.matmul(psum[0:1, 1, 0:P], ones[:, :], adjT[:, :], start=True, stop=True).then_inc(deg_psum, 1)
            pe.wait_ge(b_summed, 1)
            n = SKIPS * GATES
            pe.transpose(psum[:, 2, 0:n], b_sum[:, :], ident[0:n, 0:n]).then_inc(b_psum, 1)
            for p in range(SKIPS):
                pe.wait_ge(w_loaded[p % 2], 32 * (p // 2 + 1))
                for j in range(2):
                    if p >= 1:
                        pe.wait_ge(w_lo_ready, 2 * (p - 1) + j + 1)
                    for g in range(GATES):
                        mm = pe.transpose(psum[:, 4 + j, g * P:(g + 1) * P], w_raw[:, p % 2, j, g, :], ident[:, :])
                    mm.then_inc(w_psum, 1)

            pe.wait_ge(gnn_w_loaded, 16 * (3 + BT))
            pe.wait_ge(deg_ready, 1)
            pe.wait_ge(b_ready, 1)
            pe.wait_ge(w_lo_ready, 2 * SKIPS)
            with loop(pe, 0, gnn_iters) as it:
                for s in range(GNN_SLOTS):
                    pe.wait_ge(x_loaded[s], it * 16 + 16)
                    for b in range(BT):
                        mm = pe.matmul(psum[:, 2 * s, b * P:(b + 1) * P], x_tile[s][:, b, :], adjT[:, :], start=True, stop=True)
                    mm.then_inc(ax_psum, 1)
                for s in range(GNN_SLOTS):
                    out = psum[:, 2 * s + 1, :]
                    pe.wait_ge(h2_done, it * GNN_SLOTS + s + 1)
                    pe.matmul(out, deg_row[:, 0, :], bg0_row[:, :, :], start=True, stop=False, skip_group_check=True)
                    pe.wait_ge(axT_ready, it * GNN_SLOTS + s + 1)
                    for b in range(BT):
                        mm = pe.matmul(out[:, b * P:(b + 1) * P], axT[s][:, b * P:(b + 1) * P], wg0[:, :], start=False,
                                       stop=(b == BT - 1), skip_group_check=True)
                    mm.then_inc(h1_psum, 1)
                for s in range(GNN_SLOTS):
                    pe.wait_ge(h1_ready, it * GNN_SLOTS + s + 1)
                    for b in range(BT):
                        mm = pe.matmul(psum[:, 2 * s, b * P:(b + 1) * P], h1[s][:, b, :], adjT[:, :], start=True, stop=True)
                    mm.then_inc(ah_psum, 1)
                for s in range(GNN_SLOTS):
                    out = psum[:, 2 * s + 1, :]
                    pe.matmul(out, bg1_row[:, :], deg_row[:, :, :], start=True, stop=False)
                    pe.wait_ge(ahT_ready, it * GNN_SLOTS + s + 1)
                    pe.matmul(out, wg1[:, :], ahT[s], start=False, stop=True).then_inc(h2_psum, 1)

            pe.wait_ge(h2_done, tiles + GNN_SLOTS)
            for ph in phases:
                with loop(pe, 0, ph.iters) as it:
                    for tile, t, k, forgets in ph.body():
                        n = it * ph.per_iter + (ph.items_before + k)
                        s = k % 2
                        order = (I, G, O) if t == 0 else (F, I, G, O)
                        pe.wait_ge(gates_read, n + (CREDIT - 1))
                        if t == 0 and ph.p > 1:
                            done = phases[ph.p - 2].items_for((tile + 1) * ph.batches)
                            pe.wait_ge(h_done, done + CREDIT)
                        xh, xl = windows_at(ph, hi_bt, it, tile, t), windows_at(ph, lo_bt, it, tile, t)
                        for g in order:
                            out = psum[:, 4 * s + g, 0:ph.width]
                            wh, wl = w_hi[:, ph.p - 1, 0, g, :], w_lo[:, ph.p - 1, 0, g, :]
                            pe.matmul(out, wh, xh, start=True, stop=False)
                            pe.matmul(out, wh, xl, start=False, stop=False)
                            mm = pe.matmul(out, wl, xh, start=False, stop=(t == 0))
                            if t == 0:
                                mm.then_inc(gate_psum[g], 1)
                        if t == 0:
                            continue
                        pe.wait_ge(h_done, n + (CREDIT - 1))
                        hh, hl = hs_hi[:, s, 0:ph.width], hs_lo[:, s, 0:ph.width]
                        for g in order:
                            out = psum[:, 4 * s + g, 0:ph.width]
                            wh, wl = w_hi[:, ph.p - 1, 1, g, :], w_lo[:, ph.p - 1, 1, g, :]
                            pe.matmul(out, wh, hh, start=False, stop=False)
                            pe.matmul(out, wh, hl, start=False, stop=False)
                            pe.matmul(out, wl, hh, start=False, stop=True).then_inc(gate_psum[g], 1)

        @block.scalar
        def _(act):
            for k in range(2 * SKIPS):
                p, j = k // 2, k % 2
                act.wait_ge(w_psum, k + 1)
                act.activation(w_hi[:, p, j], psum[:, 4 + j, :].rearrange("p (g h) -> p g h", g=GATES),
                               ACT.Copy).then_inc(w_hi_ready, 1)
            with loop(act, 0, gnn_iters) as it:
                for s in range(GNN_SLOTS):
                    act.wait_ge(ax_psum, it * GNN_SLOTS + s + 1)
                    act.activation(axT[s], psum[:, 2 * s, :], ACT.Copy).then_inc(axT_ready, 1)
                for s in range(GNN_SLOTS):
                    act.wait_ge(ah_psum, it * GNN_SLOTS + s + 1)
                    act.activation(ahT[s], psum[:, 2 * s, :], ACT.Copy).then_inc(ahT_ready, 1)
                for s in range(GNN_SLOTS):
                    act.wait_ge(h2_psum, it * GNN_SLOTS + s + 1)
                    cols = bass.ds(it * (GNN_SLOTS * TW) + s * TW, TW)
                    act.activation(hT_hi[:, cols], psum[:, 2 * s + 1, :], ACT.Relu).then_inc(h2_hi, 1)

            act.wait_ge(b_ready, 1)
            act.wait_ge(h1_ready, tiles)
            for ph in phases:
                with loop(act, 0, ph.iters) as it:
                    def tanh_of(k):
                        n = it * ph.per_iter + (ph.items_before + k)
                        act.wait_ge(c_ready, n + 1)
                        act.activation(tanh_c[k % 2][:, 0:ph.width], cell[k % 2][:, 0:ph.width], ACT.Tanh).then_inc(tanh_ready, 1)

                    pending = None
                    for tile, t, k, forgets in ph.body():
                        n = it * ph.per_iter + (ph.items_before + k)
                        nf = it * ph.f_per_iter + (ph.f_before + forgets)
                        s = k % 2
                        for g in ((I, G, O) if t == 0 else (F, I, G, O)):
                            act.wait_ge(gate_psum[g], nf if g == F else n + 1)
                            if g == O:
                                act.wait_ge(h_mul, n + (CREDIT - 1))
                            b = (ph.p - 1) * GATES + g
                            op = act.activation(gate[s][g][:, 0:ph.width], psum[:, 4 * s + g, 0:ph.width],
                                                ACT.Tanh if g == G else ACT.Sigmoid, bias=bias[:, b:b + 1])
                            if g == F:
                                op.then_inc(f_ready, 1)
                            elif g == G:
                                op.then_inc(ig_ready, 1)
                            elif g == O:
                                op.then_inc(gates_read, 1)
                            if pending is not None:
                                tanh_of(pending)
                                pending = None
                        if k + 1 < ph.per_iter and (k + 1) % (2 * ph.p) < 2:
                            pending = k
                        else:
                            tanh_of(k)

        @block.vector
        def _(dve):
            dve.memset(ones[:, :], 1.0).then_inc(ones_ready, 1)
            dve.memset(start[:, 0:1], 0.0).then_inc(h2_done, GNN_SLOTS)
            dve.memset(start[:, 1:2], 0.0).then_inc(gates_read, CREDIT)
            dve.memset(start[:, 2:3], 0.0).then_inc(h_done, CREDIT)
            dve.memset(start[:, 3:4], 0.0).then_inc(h_mul, CREDIT)
            dve.wait_ge(adjT_psum, 1)
            dve.tensor_copy(adjT[:, :], psum[:, 0, 0:P]).then_inc(adjT_ready, 1)
            dve.wait_ge(b_loaded, 32)
            dve.tensor_tensor(b_sum[:, :], b_raw[:, 0, :], b_raw[:, 1, :], ALU.add).then_inc(b_summed, 1)
            dve.wait_ge(deg_psum, 1)
            for b in range(BT):
                op = dve.tensor_copy(deg_row[:, b, :], psum[0:1, 1, 0:P])
            op.then_inc(deg_ready, 1)
            dve.wait_ge(b_psum, 1)
            dve.tensor_copy(bias[:, :], psum[:, 2, 0:SKIPS * GATES]).then_inc(b_ready, 1)
            for k in range(2 * SKIPS):
                p, j = k // 2, k % 2
                dve.wait_ge(w_hi_ready, k + 1)
                dve.tensor_tensor(w_lo[:, p, j], psum[:, 4 + j, :].rearrange("p (g h) -> p g h", g=GATES),
                                  w_hi[:, p, j].bitcast(F32), ALU.subtract).then_inc(w_lo_ready, 1)
            with loop(dve, 0, gnn_iters) as it:
                for s in range(GNN_SLOTS):
                    dve.wait_ge(h1_psum, it * GNN_SLOTS + s + 1)
                    dve.tensor_scalar(h1[s], psum[:, 2 * s + 1, :].rearrange("p (b h) -> p b h", b=BT), 0.0, None,
                                      ALU.max).then_inc(h1_ready, 1)
                for s in range(GNN_SLOTS):
                    dve.wait_ge(h2_hi, it * GNN_SLOTS + s + 1)
                    cols = bass.ds(it * (GNN_SLOTS * TW) + s * TW, TW)
                    dve.scalar_tensor_tensor(out=hT_lo[:, cols], in0=psum[:, 2 * s + 1, :], scalar=0.0,
                                             in1=hT_hi[:, cols].bitcast(F32), op0=ALU.max,
                                             op1=ALU.subtract).then_inc(h2_done, 1)

            for ph in phases:
                with loop(dve, 0, ph.iters) as it:
                    def place(tile, t, k):
                        if t == ph.p - 1:
                            return (windows_at(ph, hi_bt, it, tile, t), windows_at(ph, lo_bt, it, tile, t),
                                    as_windows(ph, h_full[k % 2][:, 0:ph.width]))
                        return hs_hi[:, k % 2, 0:ph.width], hs_lo[:, k % 2, 0:ph.width], h_full[k % 2][:, 0:ph.width]

                    def split(tile, t, k):
                        n = it * ph.per_iter + (ph.items_before + k)
                        hi, lo, full = place(tile, t, k)
                        dve.wait_ge(h_mul, n + (CREDIT + 1))
                        dve.tensor_copy(hi, full).then_inc(h_hi, 1)
                        dve.wait_ge(h_hi, n + 1)
                        dve.tensor_tensor(lo, full, hi.bitcast(F32), ALU.subtract).then_inc(h_done, 1)

                    before = None
                    for tile, t, k, forgets in ph.body():
                        n = it * ph.per_iter + (ph.items_before + k)
                        nf = it * ph.f_per_iter + (ph.f_before + forgets)
                        s = k % 2
                        c = cell[s][:, 0:ph.width]
                        if t > 0:
                            dve.wait_ge(f_ready, nf)
                            dve.tensor_tensor(c, c, gate[s][F][:, 0:ph.width], ALU.mult).then_inc(fc_done, 1)
                        dve.wait_ge(ig_ready, n + 1)
                        i_g = c if t == 0 else in_gate[:, 0:ph.width]
                        op = dve.tensor_tensor(i_g, gate[s][I][:, 0:ph.width], gate[s][G][:, 0:ph.width], ALU.mult)
                        if t == 0:
                            op.then_inc(c_ready, 1)
                        else:
                            op.then_inc(ig_done, 1)
                            dve.wait_ge(fc_done, nf)
                            dve.wait_ge(ig_done, nf)
                            dve.tensor_tensor(c, c, i_g, ALU.add).then_inc(c_ready, 1)
                        if before:
                            split(*before)
                            before = None
                        dve.wait_ge(tanh_ready, n + 1)
                        dve.tensor_tensor(h_full[s][:, 0:ph.width], gate[s][O][:, 0:ph.width], tanh_c[s][:, 0:ph.width],
                                          ALU.mult).then_inc(h_mul, 1)
                        if t == ph.p - 1:
                            before = (tile, t, k)
                        else:
                            split(tile, t, k)
                    if before:
                        split(*before)


def back(nc, hT_hi, hT_lo, ident, adj_sb, psum, x, W_lin, W_val, a, W_out, src, dst, out):
    B = x.shape[0]
    tiles = B // BT
    TW = BT * P
    HEADS, DH = a.shape
    E = src.shape[0]
    EC = E // P
    GROUP = P // HEADS
    groups = B // GROUP
    pairs = GROUP // BT // 2
    GT = 2 * pairs

    with ExitStack() as ctx:
        def sb(name, shape, dt=F32):
            return ctx.enter_context(nc.sbuf_tensor(name, shape, dt))

        def sem(name):
            return ctx.enter_context(nc.semaphore(name))

        room = sb("room", [P, 8 * BANK])
        taken = [0]

        def part(width):
            taken[0] += width
            return room[:, taken[0] - width:taken[0]]

        edge_row_i = part(2 * E).bitcast(I32).rearrange("p (j e) -> p j e", j=2)
        edge_col_i = sb("edge_col_i", [P, 2, EC], I32)
        edge_row = part(2 * E).rearrange("p (j e) -> p j e", j=2)
        edge_col = sb("edge_col", [P, EC, 2])
        count_i = part(E).bitcast(I32)
        count = part(E)
        index_i = sb("index_i", [P, EC], I32)
        index = sb("index", [P, EC])
        key_row = part(E)
        key_col = sb("key_col", [P, EC])
        less = part(E)
        rank = sb("rank", [P, EC])
        permute = part(EC * E).rearrange("p (c e) -> p c e", c=EC)
        spread = part(2 * EC * P).rearrange("p (j c n) -> p j c n", j=2, c=EC)
        sorted_row = part(2 * E).rearrange("p (j e) -> p j e", j=2)
        sorted_col = sb("sorted_col", [P, EC, 2])
        at_node = sb("at_node", [P, 2, E])
        ends = sb("ends", [P, E])
        from_node = sb("from_node", [P, EC, P])
        to_node = part(EC * P).rearrange("p (c n) -> p c n", c=EC)
        adj_edge = sb("adj_edge", [P, EC])
        log_adj = sb("log_adj", [P, EC])
        log_diag = sb("log_diag", [P, EC, P])
        same_f, same_b = sb("same_f", [P, E]), sb("same_b", [P, E])
        cap_f, cap_b = sb("cap_f", [P, E]), sb("cap_b", [P, E])
        ones = sb("ones2", [P, P])
        minus_half = sb("minus_half", [P, BT])
        eps = sb("eps", [P, BT])
        start = sb("start2", [P, 8])
        w_nat = sb("w_nat", [P, 3, P])
        w_qv = sb("w_qv", [P, 2 * P])
        w_outT = sb("w_outT", [P, P])
        a_diag = sb("a_diag", [P, HEADS])
        a_relu = sb("a_relu", [P, HEADS])
        a_lin = sb("a_lin", [P, HEADS])
        w_lin_a = sb("w_lin_a", [P, HEADS])

        taken[0] = 0
        hsum = part(2 * TW).rearrange("p (s b t) -> p s b t", s=2, b=BT)
        x1T = part(2 * TW).rearrange("p (s w) -> p s w", s=2)
        relu_z = part(4 * E).rearrange("p (h b e) -> p h b e", h=2, b=2)
        xq = part(4 * P).rearrange("p (h b d) -> p h b d", h=2, b=2)
        x_res = sb("x_res", [P, 2, BT, P])
        y = sb("y", [P, 2, BT, P])
        stats = sb("stats", [P, 2, BT, 6])
        moments = sb("moments", [P, 2, BT, 2])
        var_eps = sb("var_eps", [P, 2, BT])
        rstd = sb("rstd", [P, 2, BT])
        taken[0] = 0
        va = part(2 * EC * TW).rearrange("p (s c w) -> p s c w", s=2, c=EC)
        yT = part(2 * TW).rearrange("p (s w) -> p s w", s=2)
        node_score = sb("node_score", [P, P])
        row_a, row_b, row_c, row_d = (sb(f"row_{n}", [P, E]) for n in "abcd")
        attn = sb("attn", [P, EC, P])
        score = row_d[:, :].rearrange("p (c r) -> p c r", c=EC)

        names = ("zeroed ident2_ready rows_loaded cols_loaded w_loaded a_loaded iota_done a_zero tables_f ranks "
                 "permutes spreads rows_psum rows_ready onehots adj_psum adj_done eps_done log_done diag_done sames shifted caps "
                 "wT_psum wT_ready ab_done wa_psum wa_ready ones_done credits key_done ecol_done "
                 "hsum_ready t_psum y_done stats_done moments_done var_done rstd_done x1_done x1g_ready xt_psum xT_ready "
                 "qv_psum xq_ready xv_ready z_psum rz_ready sb_open sb_psum ns_ready score_psum score_ready rows2_psum "
                 "max_f max_b shifted2 exp_done sum_f sum_b recip_done attn_row attn_psum attn_ready "
                 "vg_psum va_ready yt_psum yT_ready o_psum o_read stats2_done moments2_done var2_done rstd2_done out_ready")
        S = {n: sem("b_" + n) for n in names.split()}
        x_loaded = [sem(f"b_x_loaded{s}") for s in range(2)]
        stored = [sem(f"b_stored{s}") for s in range(2)]
        CREDIT = 2

        T_BANK, QV_BANK, Z_BANK, SCORE_BANK, ROW_BANK = 0, 2, 4, 6, 7
        VG_BANK, YT_BANK, O_BANK = 0, 4, 6
        NODE_COL = EC * P
        SUB = ALU.subtract

        x1g = sb("x1g", [P, GROUP, P])
        xvg = sb("xvg", [P, GROUP, P])

        block = ctx.enter_context(nc.Block())

        def bank2(b):
            return psum[:, b:b + 2, :]

        @block.sync
        def _(sp):
            for s in range(2):
                sp.dma_start(x_res[:, s], x[s * BT:(s + 1) * BT].rearrange("b t d -> t b d")).then_inc(x_loaded[s], 16)
            with loop(sp, 0, tiles // 2 - 1) as it:
                for s in range(2):
                    sp.wait_ge(S["y_done"], 2 * it + s + 1)
                    sp.dma_start(x_res[:, s], x[bass.ds((2 * it + 2 + s) * BT, BT)].rearrange("b t d -> t b d")).then_inc(x_loaded[s], 16)

        @block.gpsimd
        def _(pool):
            for j, e in enumerate((src, dst)):
                pool.dma_start(edge_row_i[:, j, :], e.rearrange("(a e) -> a e", a=1).broadcast_to([P, E])).then_inc(S["rows_loaded"], 16)
                pool.dma_start(edge_col_i[:, j, :], e.rearrange("(c p) -> p c", p=P), allow_slow_non_contiguous=True).then_inc(S["cols_loaded"], 16)
            for j, w in enumerate((W_lin, W_val, W_out)):
                pool.dma_start(w_nat[:, j, :], w).then_inc(S["w_loaded"], 16)
            pool.memset(a_diag[:, :], 0.0).then_inc(S["a_zero"], 1)
            pool.iota(count_i[:, :], pattern=[[1, E]], base=0, channel_multiplier=0).then_inc(S["iota_done"], 1)
            pool.iota(index_i[:, :], pattern=[[P, EC]], base=0, channel_multiplier=1).then_inc(S["iota_done"], 1)
            pool.wait_ge(S["a_zero"], 1)
            for h in range(HEADS):
                pool.dma_start(a_diag[h * DH:(h + 1) * DH, h:h + 1], a[h].rearrange("(d o) -> d o", o=1), allow_slow_non_contiguous=True).then_inc(S["a_loaded"], 16)

            def rstd_of(s, ready, var_sem, done_sem, n):
                pool.wait_ge(ready, n + 1)
                pool.tensor_tensor(var_eps[:, s, :], moments[:, s, :, 1], eps[:, :], ALU.add).then_inc(var_sem, 1)
                pool.wait_ge(var_sem, n + 1)
                pool.tensor_tensor(rstd[:, s, :], var_eps[:, s, :], minus_half[:, :], ALU.pow).then_inc(done_sem, 1)

            pool.wait_ge(S["diag_done"], EC)
            with loop(pool, 0, groups) as g:
                with loop(pool, 0, pairs) as j:
                    k0 = g * GT + 2 * j
                    for s in range(2):
                        cols = bass.ds((g * GT + 2 * j + s) * TW, TW)
                        pool.wait_ge(S["t_psum"], k0 + s + 1)
                        pool.tensor_tensor(hsum[:, s].rearrange("p b t -> p (b t)"), hT_hi[:, cols].bitcast(F32),
                                           hT_lo[:, cols].bitcast(F32), ALU.add).then_inc(S["hsum_ready"], 1)
                    for s in range(2):
                        rstd_of(s, S["moments_done"], S["var_done"], S["rstd_done"], k0 + s)
                    for s in range(2):
                        pool.wait_ge(S["x1_done"], k0 + s + 1)
                        pool.tensor_copy(x1g[:, bass.ds((2 * j + s) * BT, BT), :], y[:, s]).then_inc(S["x1g_ready"], 1)
                with loop(pool, 0, pairs) as j:
                    for s in range(2):
                        rstd_of(s, S["moments2_done"], S["var2_done"], S["rstd2_done"], g * GT + 2 * j + s)

        @block.tensor
        def _(pe):
            pe.wait_ge(S["w_loaded"], 48)
            for j in range(3):
                mm = pe.transpose(psum[:, 0, j * P:(j + 1) * P], w_nat[:, j, :], ident[:, :])
            mm.then_inc(S["wT_psum"], 1)
            pe.wait_ge(S["ab_done"], 2)
            pe.matmul(psum[:, 1, 0:HEADS], w_nat[:, 0, :], a_lin[:, :], start=True, stop=True).then_inc(S["wa_psum"], 1)
            pe.wait_ge(S["permutes"], EC)
            pe.wait_ge(S["spreads"], 2 * EC)
            for j in range(2):
                for c in range(EC):
                    pe.matmul(psum[:, 2, j * E:(j + 1) * E], spread[:, j, c, :], permute[:, c, :], start=(c == 0), stop=(c == EC - 1))
            for r in range(EC):
                for c in range(EC):
                    mm = pe.matmul(psum[:, 3, 2 * r:2 * r + 2], permute[:, c, r * P:(r + 1) * P], edge_col[:, c, :],
                                   start=(c == 0), stop=(c == EC - 1))
            mm.then_inc(S["rows_psum"], 1)
            pe.wait_ge(S["onehots"], 2)
            for c in range(EC):
                mm = pe.matmul(psum[:, 4, c * P:(c + 1) * P], at_node[:, 0, c * P:(c + 1) * P], adj_sb[:, :], start=True, stop=True)
            mm.then_inc(S["adj_psum"], 1)
            pe.wait_ge(S["diag_done"], EC)
            pe.wait_ge(S["wT_ready"], 2)
            pe.wait_ge(S["wa_ready"], 1)
            pe.wait_ge(S["ab_done"], 2)
            pe.wait_ge(S["caps"], 2)

            def half_range(h):
                return range(2 * h, 2 * h + 2)

            def project(k0, s, h):
                pe.wait_ge(S["xv_ready"], (k0 + s) * 2 + h + 1)
                for b in half_range(h):
                    mm = pe.matmul(psum[:, QV_BANK + h, (b % 2) * 2 * P:(b % 2 + 1) * 2 * P], x1T[:, s, b * P:(b + 1) * P],
                                   w_qv[:, :], start=True, stop=True)
                mm.then_inc(S["qv_psum"], 1)

            def node_scores(j, s):
                for b in range(BT):
                    col = ((2 * j + s) * BT + b) * HEADS + NODE_COL
                    pe.matmul(psum[:, SCORE_BANK, bass.ds(col, HEADS)], x1T[:, s, b * P:(b + 1) * P], w_lin_a[:, :],
                              start=False, stop=True, skip_group_check=True)

            def gather(k0, s, h):
                pe.wait_ge(S["xq_ready"], (k0 + s) * 2 + h + 1)
                for b in range(2):
                    mm = pe.matmul(psum[:, Z_BANK + h, b * E:(b + 1) * E], xq[:, h, b, :], ends[:, :], start=True, stop=True)
                mm.then_inc(S["z_psum"], 1)

            def edge_scores(k0, j, s, h):
                pe.wait_ge(S["rz_ready"], (k0 + s) * 2 + h + 1)
                for b in half_range(h):
                    for c in range(EC):
                        col = ((2 * j + s) * BT + b) * HEADS + c * P
                        mm = pe.matmul(psum[:, SCORE_BANK, bass.ds(col, HEADS)], relu_z[:, h, b % 2, c * P:(c + 1) * P],
                                       a_relu[:, :], start=False, stop=True, skip_group_check=True)
                return mm

            with loop(pe, 0, groups) as g:
                pe.wait_ge(S["o_read"], g * GT + CREDIT)
                for c in range(EC):
                    pe.matmul(psum[:, SCORE_BANK, c * P:(c + 1) * P], log_diag[:, c, :], ones[:, :], start=(c == 0), stop=True,
                              skip_group_check=True)
                with loop(pe, 0, pairs) as j:
                    k0 = g * GT + 2 * j
                    for s in range(2):
                        pe.wait_ge(S["hsum_ready"], k0 + s + 1)
                        for b in range(BT):
                            mm = pe.transpose(psum[:, T_BANK + s, b * P:(b + 1) * P], hsum[:, s, b, :], ident[:, :])
                        mm.then_inc(S["t_psum"], 1)
                    for s in range(2):
                        pe.wait_ge(S["x1_done"], k0 + s + 1)
                        for b in range(BT):
                            mm = pe.transpose(psum[:, T_BANK + s, b * P:(b + 1) * P], y[:, s, b, :], ident[:, :])
                        mm.then_inc(S["xt_psum"], 1)
                    pe.wait_ge(S["xT_ready"], k0 + 1)
                    project(k0, 0, 0)
                    project(k0, 0, 1)
                    node_scores(j, 0)
                    gather(k0, 0, 0)
                    pe.wait_ge(S["xT_ready"], k0 + 2)
                    project(k0, 1, 0)
                    gather(k0, 0, 1)
                    edge_scores(k0, j, 0, 0)
                    project(k0, 1, 1)
                    gather(k0, 1, 0)
                    edge_scores(k0, j, 0, 1)
                    node_scores(j, 1)
                    gather(k0, 1, 1)
                    edge_scores(k0, j, 1, 0)
                    edge_scores(k0, j, 1, 1).then_inc(S["sb_psum"], 1)
                pe.wait_ge(S["ns_ready"], g + 1)
                for c in range(EC):
                    mm = pe.matmul(psum[:, SCORE_BANK, c * P:(c + 1) * P], ends[:, c * P:(c + 1) * P], node_score[:, :],
                                   start=False, stop=True, skip_group_check=True)
                mm.then_inc(S["score_psum"], 1)
                pe.wait_ge(S["score_ready"], g + 1)
                for c in range(EC):
                    mm = pe.transpose(psum[:, ROW_BANK, c * P:(c + 1) * P], score[:, c, :], ident[:, :])
                mm.then_inc(S["rows2_psum"], 1)
                pe.wait_ge(S["attn_row"], g + 1)
                for c in range(EC):
                    mm = pe.transpose(psum[:, ROW_BANK, c * P:(c + 1) * P], row_a[:, c * P:(c + 1) * P], ident[:, :])
                mm.then_inc(S["attn_psum"], 1)
                with loop(pe, 0, pairs) as j:
                    k0 = g * GT + 2 * j
                    for s in range(2):
                        pe.wait_ge(S["attn_ready"], g + 1)
                        for c in range(EC):
                            mm = pe.matmul(psum[:, VG_BANK + 2 * s + c, :], at_node[:, 1, c * P:(c + 1) * P],
                                           xvg[:, bass.ds((2 * j + s) * BT, BT), :], start=True, stop=True)
                        mm.then_inc(S["vg_psum"], 1)
                    for s in range(2):
                        pe.wait_ge(S["va_ready"], k0 + s + 1)
                        for b in range(BT):
                            for c in range(EC):
                                mm = pe.matmul(psum[:, YT_BANK + s, b * P:(b + 1) * P], va[:, s, c, b * P:(b + 1) * P],
                                               from_node[:, c, :], start=(c == 0), stop=(c == EC - 1))
                        mm.then_inc(S["yt_psum"], 1)
                    for s in range(2):
                        pe.wait_ge(S["yT_ready"], k0 + s + 1)
                        pe.wait_ge(S["o_read"], k0 + s + 1)
                        for b in range(BT):
                            mm = pe.matmul(psum[:, O_BANK + s, b * P:(b + 1) * P], yT[:, s, b * P:(b + 1) * P], w_outT[:, :],
                                           start=True, stop=True)
                        mm.then_inc(S["o_psum"], 1)

        @block.scalar
        def _(act):
            act.wait_ge(S["eps_done"], 1)
            act.activation(log_adj[:, :], adj_edge[:, :], ACT.Ln).then_inc(S["log_done"], 1)
            with loop(act, 0, groups) as g:
                with loop(act, 0, pairs) as j:
                    k0 = g * GT + 2 * j

                    def query(s, h):
                        act.wait_ge(S["qv_psum"], (k0 + s) * 2 + h + 1)
                        act.activation(xq[:, h], psum[:, QV_BANK + h, :].rearrange("p (b w) -> p b w", b=2)[:, :, 0:P],
                                       ACT.Copy).then_inc(S["xq_ready"], 1)

                    def relu(s, h):
                        act.wait_ge(S["z_psum"], (k0 + s) * 2 + h + 1)
                        act.activation(relu_z[:, h], psum[:, Z_BANK + h, :].rearrange("p (b e) -> p b e", b=2),
                                       ACT.Relu).then_inc(S["rz_ready"], 1)

                    for s in range(2):
                        act.wait_ge(S["xt_psum"], k0 + s + 1)
                        act.activation(x1T[:, s, :], psum[:, T_BANK + s, :], ACT.Copy).then_inc(S["xT_ready"], 1)
                    query(0, 0)
                    query(0, 1)
                    relu(0, 0)
                    query(1, 0)
                    relu(0, 1)
                    query(1, 1)
                    relu(1, 0)
                    relu(1, 1)
                act.wait_ge(S["shifted2"], g + 1)
                act.activation(row_d[:, :], row_c[:, :], ACT.Exp).then_inc(S["exp_done"], 1)
                with loop(act, 0, pairs) as j:
                    for s in range(2):
                        act.wait_ge(S["yt_psum"], g * GT + 2 * j + s + 1)
                        act.activation(yT[:, s, :], psum[:, YT_BANK + s, :], ACT.Copy).then_inc(S["yT_ready"], 1)
                    for s in range(2):
                        act.wait_ge(S["out_ready"], g * GT + 2 * j + s + 1)
                        tile = out[bass.ds((g * GT + 2 * j + s) * BT, BT)]
                        act.dma_start(tile.rearrange("b t d -> t b d"), y[:, s]).then_inc(stored[s], 16)
            for s in range(2):
                act.wait_ge(stored[s], 16 * (tiles // 2 + 1))

        @block.vector
        def _(dve):
            dve.memset(ones[:, :], 1.0).then_inc(S["ones_done"], 1)
            dve.memset(minus_half[:, :], -0.5).then_inc(S["ones_done"], 1)
            dve.memset(eps[:, :], LN_EPS).then_inc(S["ones_done"], 1)
            for n, (name, by) in enumerate((("t_psum", CREDIT), ("x1g_ready", CREDIT), ("xv_ready", CREDIT), ("o_read", CREDIT))):
                dve.memset(start[:, n:n + 1], 0.0).then_inc(S[name], by)
            for s in range(2):
                dve.memset(start[:, 4 + s:5 + s], 0.0).then_inc(stored[s], 16)

            dve.wait_ge(S["a_loaded"], 16 * HEADS)
            dve.tensor_scalar(a_lin[:, :], a_diag[:, :], SLOPE, None, ALU.mult).then_inc(S["ab_done"], 1)
            dve.tensor_scalar(a_relu[:, :], a_diag[:, :], 1.0 - SLOPE, None, ALU.mult).then_inc(S["ab_done"], 1)
            dve.wait_ge(S["wT_psum"], 1)
            dve.tensor_copy(w_qv[:, :], psum[:, 0, 0:2 * P]).then_inc(S["wT_ready"], 1)
            dve.tensor_copy(w_outT[:, :], psum[:, 0, 2 * P:3 * P]).then_inc(S["wT_ready"], 1)
            dve.wait_ge(S["wa_psum"], 1)
            dve.tensor_copy(w_lin_a[:, :], psum[:, 1, 0:HEADS]).then_inc(S["wa_ready"], 1)

            dve.wait_ge(S["rows_loaded"], 32)
            dve.tensor_copy(edge_row, edge_row_i).then_inc(S["tables_f"], 1)
            dve.wait_ge(S["cols_loaded"], 32)
            for j in range(2):
                dve.tensor_copy(edge_col[:, :, j], edge_col_i[:, j, :]).then_inc(S["ecol_done"], 1)
            dve.wait_ge(S["iota_done"], 2)
            dve.tensor_copy(count[:, :], count_i[:, :]).then_inc(S["tables_f"], 1)
            dve.tensor_copy(index[:, :], index_i[:, :]).then_inc(S["tables_f"], 1)
            dve.wait_ge(S["tables_f"], 3)
            dve.wait_ge(S["ecol_done"], 2)
            dve.scalar_tensor_tensor(out=key_row[:, :], in0=edge_row[:, 0, :], scalar=float(E), in1=count[:, :],
                                     op0=ALU.mult, op1=ALU.add).then_inc(S["key_done"], 1)
            dve.scalar_tensor_tensor(out=key_col[:, :], in0=edge_col[:, :, 0], scalar=float(E), in1=index[:, :],
                                     op0=ALU.mult, op1=ALU.add).then_inc(S["key_done"], 1)
            for c in range(EC):
                for j in range(2):
                    dve.tensor_scalar(spread[:, j, c, :], ones[:, :], edge_col[:, c, j:j + 1], None, ALU.mult).then_inc(S["spreads"], 1)
            dve.wait_ge(S["key_done"], 2)
            for c in range(EC):
                if c:
                    dve.wait_ge(S["ranks"], c)
                dve.tensor_scalar(less[:, :], key_row[:, :], key_col[:, c:c + 1], 0.0, ALU.is_lt, ALU.add,
                                  accum_out=rank[:, c:c + 1]).then_inc(S["ranks"], 1)
            dve.wait_ge(S["ranks"], EC)
            for c in range(EC):
                dve.tensor_scalar(permute[:, c, :], count[:, :], rank[:, c:c + 1], None, ALU.is_equal).then_inc(S["permutes"], 1)
            dve.wait_ge(S["rows_psum"], 1)
            dve.tensor_copy(sorted_row, psum[:, 2, :].rearrange("p (j e) -> p j e", j=2)).then_inc(S["rows_ready"], 1)
            dve.tensor_copy(sorted_col[:, :, :], psum[:, 3, 0:2 * EC].rearrange("p (c j) -> p c j", j=2)).then_inc(S["rows_ready"], 1)
            dve.memset(same_f[:, 0:1], 0.0)
            dve.memset(same_b[:, E - 1:E], 0.0).then_inc(S["rows_ready"], 1)
            dve.wait_ge(S["rows_ready"], 3)
            for j in range(2):
                dve.tensor_scalar(at_node[:, j, :], sorted_row[:, j, :], index[:, 0:1], None, ALU.is_equal).then_inc(S["onehots"], 1)
            for j, of_edge in enumerate((from_node, to_node)):
                for c in range(EC):
                    op = dve.tensor_scalar(of_edge[:, c, :], count[:, 0:P], sorted_col[:, c, j:j + 1], None, ALU.is_equal)
            op.then_inc(S["onehots"], 1)
            dve.wait_ge(S["onehots"], 3)
            dve.tensor_tensor(ends[:, :], at_node[:, 0, :], at_node[:, 1, :], ALU.add)
            dve.tensor_tensor(same_f[:, 1:E], sorted_row[:, 0, 1:E], sorted_row[:, 0, 0:E - 1], ALU.is_equal)
            dve.tensor_tensor(same_b[:, 0:E - 1], sorted_row[:, 0, 1:E], sorted_row[:, 0, 0:E - 1], ALU.is_equal).then_inc(S["sames"], 1)
            dve.wait_ge(S["sames"], 1)
            for same, cap in ((same_f, row_a), (same_b, row_b)):
                dve.tensor_scalar(cap[:, :], same[:, :], 2.0, -1.0, ALU.mult, ALU.add).then_inc(S["shifted"], 1)
            dve.wait_ge(S["shifted"], 2)
            for sign, cap in ((row_a, cap_f), (row_b, cap_b)):
                dve.tensor_scalar(cap[:, :], sign[:, :], FLT_MAX, None, ALU.mult).then_inc(S["caps"], 1)
            dve.wait_ge(S["adj_psum"], 1)
            for c in range(EC):
                if c:
                    dve.wait_ge(S["adj_done"], c)
                dve.tensor_tensor_reduce(less[:, 0:P], psum[:, 4, c * P:(c + 1) * P], to_node[:, c, :], 1.0, 0.0,
                                         ALU.mult, ALU.add, rank[:, c:c + 1]).then_inc(S["adj_done"], 1)
            dve.wait_ge(S["adj_done"], EC)
            dve.tensor_scalar(adj_edge[:, :], rank[:, :], LOG_EPS, None, ALU.add).then_inc(S["eps_done"], 1)
            dve.wait_ge(S["log_done"], 1)
            for c in range(EC):
                dve.tensor_scalar(log_diag[:, c, :], ident[:, :], log_adj[:, c:c + 1], None, ALU.mult).then_inc(S["diag_done"], 1)

            def moments_of(s, st_sem, mo_sem, n):
                for b in range(BT):
                    op = dve.bn_stats(stats[:, s, b, :], y[:, s, b, :])
                op.then_inc(st_sem, 1)
                dve.wait_ge(st_sem, n + 1)
                dve.memset(start[:, 7:8], 0.0)
                for b in range(BT):
                    op = dve.bn_aggr(moments[:, s, b, :], stats[:, s, b, :])
                op.then_inc(mo_sem, 1)

            def normalize(s, rstd_sem, n):
                dve.wait_ge(rstd_sem, n + 1)
                for b in range(BT):
                    op = dve.tensor_scalar(y[:, s, b, :], y[:, s, b, :], moments[:, s, b, 0:1], rstd[:, s, b:b + 1],
                                           SUB, ALU.mult)
                return op

            with loop(dve, 0, groups) as g:
                with loop(dve, 0, pairs) as j:
                    k0 = g * GT + 2 * j
                    for s in range(2):
                        dve.wait_ge(S["t_psum"], k0 + s + CREDIT + 1)
                        dve.wait_ge(stored[s], g * (16 * pairs) + 16)
                        dve.wait_ge(x_loaded[s], (g * pairs + j) * 16 + 16)
                        dve.wait_ge(S["x1g_ready"], k0 + s + 1)
                        dve.tensor_tensor(y[:, s], psum[:, T_BANK + s, :].rearrange("p (b d) -> p b d", b=BT), x_res[:, s],
                                          ALU.add).then_inc(S["y_done"], 1)
                        dve.wait_ge(S["y_done"], k0 + s + 1)
                        moments_of(s, S["stats_done"], S["moments_done"], k0 + s)
                    for s in range(2):
                        normalize(s, S["rstd_done"], k0 + s).then_inc(S["x1_done"], 1)
                    for s in range(2):
                        for h in range(2):
                            dve.wait_ge(S["qv_psum"], (k0 + s) * 2 + h + 1)
                            dve.wait_ge(S["xq_ready"], (k0 + s) * 2 + h + 1)
                            dve.tensor_copy(xvg[:, bass.ds((2 * j + s) * BT + 2 * h, 2), :],
                                            psum[:, QV_BANK + h, :].rearrange("p (b w) -> p b w", b=2)[:, :, P:2 * P])\
                               .then_inc(S["xv_ready"], 1)
                dve.wait_ge(S["x1g_ready"], (g + 1) * GT + CREDIT)
                dve.wait_ge(S["sb_psum"], (g + 1) * pairs)
                dve.tensor_copy(node_score[:, :], psum[:, SCORE_BANK, NODE_COL:NODE_COL + P]).then_inc(S["ns_ready"], 1)
                dve.wait_ge(S["score_psum"], g + 1)
                dve.tensor_copy(score, psum[:, SCORE_BANK, 0:EC * P].rearrange("p (c r) -> p c r", c=EC)).then_inc(S["score_ready"], 1)
                dve.wait_ge(S["rows2_psum"], g + 1)
                edges = psum[:, ROW_BANK, 0:E]
                dve.tensor_tensor_scan(row_a[:, :], cap_f[:, :], edges, -FLT_MAX, ALU.min, ALU.max).then_inc(S["max_f"], 1)
                dve.wait_ge(S["max_f"], g + 1)
                dve.tensor_tensor_scan(row_b[:, ::-1], cap_b[:, ::-1], row_a[:, ::-1], -FLT_MAX, ALU.min, ALU.max).then_inc(S["max_b"], 1)
                dve.wait_ge(S["max_b"], g + 1)
                dve.tensor_tensor(row_c[:, :], edges, row_b[:, :], SUB).then_inc(S["shifted2"], 1)
                dve.wait_ge(S["exp_done"], g + 1)
                dve.tensor_tensor_scan(row_a[:, :], same_f[:, :], row_d[:, :], 0.0, ALU.mult, ALU.add).then_inc(S["sum_f"], 1)
                dve.wait_ge(S["sum_f"], g + 1)
                dve.tensor_tensor_scan(row_b[:, ::-1], cap_b[:, ::-1], row_a[:, ::-1], 0.0, ALU.min, ALU.max).then_inc(S["sum_b"], 1)
                dve.wait_ge(S["sum_b"], g + 1)
                dve.reciprocal(row_c[:, :], row_b[:, :]).then_inc(S["recip_done"], 1)
                dve.wait_ge(S["recip_done"], g + 1)
                dve.tensor_tensor(row_a[:, :], row_d[:, :], row_c[:, :], ALU.mult).then_inc(S["attn_row"], 1)
                dve.wait_ge(S["attn_psum"], g + 1)
                dve.tensor_copy(attn[:, :, :], psum[:, ROW_BANK, 0:EC * P].rearrange("p (c r) -> p c r", c=EC)).then_inc(S["attn_ready"], 1)
                with loop(dve, 0, pairs) as j:
                    k0 = g * GT + 2 * j
                    for s in range(2):
                        dve.wait_ge(S["attn_ready"], g + 1)
                        dve.wait_ge(S["vg_psum"], k0 + s + 1)
                        for c in range(EC):
                            w = attn[:, c, bass.ds((2 * j + s) * BT * HEADS, BT * HEADS)]
                            op = dve.tensor_tensor(va[:, s, c, :].rearrange("p (r d) -> p r d", d=DH),
                                                   psum[:, VG_BANK + 2 * s + c, :].rearrange("p (r d) -> p r d", d=DH),
                                                   w.unsqueeze(2).broadcast_to([P, BT * HEADS, DH]), ALU.mult)
                        op.then_inc(S["va_ready"], 1)
                    for s in range(2):
                        dve.wait_ge(S["o_psum"], k0 + s + 1)
                        dve.wait_ge(stored[s], (g * pairs + j) * 16 + 16)
                        dve.tensor_tensor(y[:, s], psum[:, O_BANK + s, :].rearrange("p (b d) -> p b d", b=BT),
                                          x1g[:, bass.ds((2 * j + s) * BT, BT), :], ALU.add).then_inc(S["o_read"], 1)
                        dve.wait_ge(S["o_read"], k0 + s + CREDIT + 1)
                        moments_of(s, S["stats2_done"], S["moments2_done"], k0 + s)
                    for s in range(2):
                        normalize(s, S["rstd2_done"], k0 + s).then_inc(S["out_ready"], 1)


def program(nc, x, adj, Wg0, bg0, Wg1, bg1, Wih, Whh, bih, bhh, W_lin, W_val, a, W_out, src, dst, out):
    B = x.shape[0]
    with ExitStack() as ctx:
        hT_hi = ctx.enter_context(nc.sbuf_tensor("hT_hi", [P, B * P], F32R))
        hT_lo = ctx.enter_context(nc.sbuf_tensor("hT_lo", [P, B * P], F32R))
        ident = ctx.enter_context(nc.sbuf_tensor("ident", [P, P], F32))
        adj_sb = ctx.enter_context(nc.sbuf_tensor("adj_sb", [P, P], F32))
        psum = ctx.enter_context(nc.psum_tensor("psum", [P, 8, BANK], F32))
        front(nc, hT_hi, hT_lo, ident, adj_sb, psum, x, adj, Wg0, bg0, Wg1, bg1, Wih, Whh, bih, bhh)
        back(nc, hT_hi, hT_lo, ident, adj_sb, psum, x, W_lin, W_val, a, W_out, src, dst, out)


_INPUTS = ("x", "adj", "L0_gnn_Wg0", "L0_gnn_bg0", "L0_gnn_Wg1", "L0_gnn_bg1", "L0_gnn_Wih", "L0_gnn_Whh", "L0_gnn_bih",
           "L0_gnn_bhh", "L1_gnn_W_lin", "L1_gnn_W_val", "L1_gnn_a", "L1_gnn_W_out", "L1_gnn_src", "L1_gnn_dst")


def kernel(**inputs):
    import numpy as np
    import concourse.bacc as bacc
    from concourse.bass_utils import run_bass_kernel_spmd

    nc = bacc.Bacc("TRN2", target_bir_lowering=False, num_devices=1)
    arrays, args = {}, []
    for name in _INPUTS:
        array = np.ascontiguousarray(inputs[name])
        arrays[name] = array
        args.append(nc.dram_tensor(name, array.shape, mybir.dt.from_np(array.dtype), kind="ExternalInput").ap())
    args.append(nc.dram_tensor("out", arrays["x"].shape, F32, kind="ExternalOutput").ap())
    program(nc, *args)
    return run_bass_kernel_spmd(nc, [arrays], core_ids=[0]).results[0]["out"]
```

```python
from contextlib import ExitStack

import concourse.bass as bass
from concourse import mybir
from concourse.alu_op_type import AluOpType as ALU

F32 = mybir.dt.float32
F32R = mybir.dt.float32r
I32 = mybir.dt.int32
ACT = mybir.ActivationFunctionType
AX = mybir.AxisListType

P = 128
BANK = 512
SKIPS = 4
GATES = 4
I, F, G, O = range(GATES)
LN_EPS = 1e-5
LOG_EPS = 1e-8
SLOPE = 0.2
FLT_MAX = 3.4028234e38

BT = 4
GNN_SLOTS = 4


def loop(engine, first, end):
    return engine.bass.Fori(first, end, engines=(engine.engine,), hint_back_edge=True)


class LstmPhase:

    def __init__(self, p, batches, pairs, n_batch, items_before, f_before):
        self.p, self.batches, self.pairs = p, batches, pairs
        self.windows = P // p
        self.width = batches * self.windows
        self.iters = n_batch // (batches * 2 * pairs)
        self.per_iter = 2 * p * pairs
        self.f_per_iter = 2 * (p - 1) * pairs
        self.items_before, self.f_before = items_before, f_before
        self.items_after = items_before + self.iters * self.per_iter
        self.f_after = f_before + self.iters * self.f_per_iter

    def body(self):
        forgets = 0
        for pair in range(self.pairs):
            for t in range(self.p):
                for s in range(2):
                    forgets += t > 0
                    yield 2 * pair + s, t, 2 * (pair * self.p + t) + s, forgets

    def items_for(self, batches):
        tile = -(-batches // self.batches) - 1
        return self.items_before + 2 * self.p * (tile // 2) + 2 * (self.p - 1) + tile % 2 + 1


def lstm_phases(n_batch):
    phases, items, forgets = [], 0, 0
    for p, batches, pairs in ((1, 4, 4), (2, 8, 2), (3, 8, 2), (4, 16, 2)):
        phases.append(LstmPhase(p, batches, pairs, n_batch, items, forgets))
        items, forgets = phases[-1].items_after, phases[-1].f_after
    return phases


def front(nc, hT_hi, hT_lo, ident, adj_sb, psum, x, adj, Wg0, bg0, Wg1, bg1, Wih, Whh, bih, bhh):
    B = x.shape[0]
    tiles = B // BT
    gnn_iters = tiles // GNN_SLOTS
    phases = lstm_phases(B)
    TW = BT * P
    DEG_LO, BIAS_LO = 32, 64
    RANKS = BIAS_LO + 1

    with ExitStack() as ctx:
        def sb(name, shape, dt=F32):
            return ctx.enter_context(nc.sbuf_tensor(name, shape, dt))

        def sem(name):
            return ctx.enter_context(nc.semaphore(name))

        adjT = sb("adjT", [P, P])
        wg0 = sb("wg0", [P, P])
        wg1_hi = sb("wg1_hi", [P, P], F32R)
        wg1_lo = sb("wg1_lo", [P, P], F32R)
        ones = sb("ones", [P, RANKS])
        start = sb("start", [P, 4])
        deg_rows = sb("deg_rows", [RANKS, BT, P], F32R)
        bg0_rows = sb("bg0_rows", [RANKS, BT, P], F32R)
        bg1_rows = sb("bg1_rows", [RANKS, P], F32R)
        w_hi = sb("w_hi", [P, SKIPS, 2, GATES, P], F32R)
        w_lo = sb("w_lo", [P, SKIPS, 2, GATES, P], F32R)
        b_raw = sb("b_raw", [SKIPS * GATES, 2, P])
        b_sum = sb("b_sum", [SKIPS * GATES, P])
        bias = sb("bias", [P, SKIPS * GATES])

        work = sb("work", [P, 15, BANK])
        axT = [work[:, s, :] for s in range(GNN_SLOTS)]
        h1 = [work[:, 4 + s, :].rearrange("p (b h) -> p b h", b=BT) for s in range(GNN_SLOTS)]
        x_tile = [work[:, 8 + s, :].rearrange("p (b d) -> p b d", b=BT) for s in range(GNN_SLOTS)]
        wg1 = work[:, 12, 0:P]
        bg0_raw = work[0:RANKS, 13, :].rearrange("p (b h) -> p b h", b=BT)
        bg1_raw = work[0:RANKS, 12, P:2 * P]
        w_raw = work[:, 0:4, :].rearrange("p (r j) (g d) -> p r j g d", r=2, g=GATES)
        gate = [[work[:, 4 * s + g, :] for g in range(GATES)] for s in range(2)]
        cell = [work[:, 8 + s, :] for s in range(2)]
        in_gate = work[:, 10, :]
        tanh_c = [work[:, 11 + s, :] for s in range(2)]
        h_full = [work[:, 13 + s, :] for s in range(2)]
        hs_hi = sb("hs_hi", [P, 2, BANK], F32R)
        hs_lo = sb("hs_lo", [P, 2, BANK], F32R)

        ident_zero, ident_ready = sem("ident_zero"), sem("ident_ready")
        ones_ready = sem("ones_ready")
        adj_loaded, gnn_w_loaded, b_loaded = sem("adj_loaded"), sem("gnn_w_loaded"), sem("b_loaded")
        w_loaded = [sem(f"w_loaded{i}") for i in range(2)]
        x_loaded = [sem(f"x_loaded{s}") for s in range(GNN_SLOTS)]
        adjT_psum, adjT_ready, deg_psum, deg_ready = (sem(n) for n in ("adjT_psum", "adjT_ready", "deg_psum", "deg_ready"))
        b_summed, b_psum, b_ready = sem("b_summed"), sem("b_psum"), sem("b_ready")
        w_psum, w_hi_ready, w_lo_ready = sem("w_psum"), sem("w_hi_ready"), sem("w_lo_ready")
        ax_psum, axT_ready = sem("ax_psum"), sem("axT_ready")
        h1_psum, h1_ready = sem("h1_psum"), sem("h1_ready")
        ah_psum, ahT_hi, ahT_ready = sem("ah_psum"), sem("ahT_hi"), sem("ahT_ready")
        bias_hi, bias_rows_ready, wg1_cut, wg1_ready = sem("bias_hi"), sem("bias_rows_ready"), sem("wg1_cut"), sem("wg1_ready")
        deg_hi = sem("deg_hi")
        h2_psum, h2_hi, h2_done = sem("h2_psum"), sem("h2_hi"), sem("h2_done")
        gate_psum = [sem(f"gate_psum_{n}") for n in "ifgo"]
        gates_read = sem("gates_read")
        f_ready, ig_ready, tanh_ready = sem("f_ready"), sem("ig_ready"), sem("tanh_ready")
        fc_done, ig_done, c_ready = sem("fc_done"), sem("ig_done"), sem("c_ready")
        h_mul, h_hi, h_done = sem("h_mul"), sem("h_hi"), sem("h_done")
        CREDIT = 2

        hi_bt = hT_hi[:, :].rearrange("p (b t) -> p b t", t=P)
        lo_bt = hT_lo[:, :].rearrange("p (b t) -> p b t", t=P)

        def windows_at(ph, view, it, tile, t):
            first = (it * (2 * ph.pairs) + tile) * ph.batches
            return view[:, bass.ds(first, ph.batches), t:t + (ph.windows - 1) * ph.p + 1:ph.p]

        def as_windows(ph, flat):
            return flat.rearrange("p (b w) -> p b w", b=ph.batches)

        block = ctx.enter_context(nc.Block())

        @block.sync
        def _(sp):
            sp.dma_start(adj_sb[:, :], adj).then_inc(adj_loaded, 16)
            sp.dma_start(wg0[:, :], Wg0).then_inc(gnn_w_loaded, 16)
            sp.dma_start(wg1, Wg1).then_inc(gnn_w_loaded, 16)
            for b in range(BT):
                sp.dma_start(bg0_raw[:, b, :], bg0.rearrange("(a h) -> a h", a=1).broadcast_to([RANKS, P])).then_inc(gnn_w_loaded, 16)
            sp.dma_start(bg1_raw, bg1.rearrange("(a h) -> a h", a=1).broadcast_to([RANKS, P])).then_inc(gnn_w_loaded, 16)
            sp.dma_start(b_raw[:, 0, :], bih.rearrange("s (g h) -> (s g) h", g=GATES)).then_inc(b_loaded, 16)
            sp.dma_start(b_raw[:, 1, :], bhh.rearrange("s (g h) -> (s g) h", g=GATES)).then_inc(b_loaded, 16)
            for s in range(GNN_SLOTS):
                sp.dma_start(x_tile[s], x[s * BT:(s + 1) * BT].rearrange("b t d -> t b d")).then_inc(x_loaded[s], 16)
            with loop(sp, 0, gnn_iters - 1) as it:
                for s in range(GNN_SLOTS):
                    sp.wait_ge(ax_psum, it * GNN_SLOTS + s + 1)
                    src = x[bass.ds((it * GNN_SLOTS + GNN_SLOTS + s) * BT, BT)]
                    sp.dma_start(x_tile[s], src.rearrange("b t d -> t b d")).then_inc(x_loaded[s], 16)

        @block.gpsimd
        def _(pool):
            pool.memset(ident[:, :], 0.0).then_inc(ident_zero, 1)
            pool.wait_ge(ident_zero, 1)
            pool.affine_select(out=ident[:, :], in_=ident[:, :], compare_op=ALU.not_equal, fill=1.0, base=0,
                               pattern=[[-1, P]], channel_multiplier=1).then_inc(ident_ready, 1)
            for p in range(SKIPS):
                if p >= 2:
                    pool.wait_ge(w_psum, 2 * (p - 1))
                for j, w in enumerate((Wih, Whh)):
                    pool.dma_start(w_raw[:, p % 2, j], w[p].rearrange("(g h) d -> h g d", g=GATES)).then_inc(w_loaded[p % 2], 16)

        @block.tensor
        def _(pe):
            pe.wait_ge(adj_loaded, 16)
            pe.wait_ge(ident_ready, 1)
            pe.transpose(psum[:, 0, 0:P], adj_sb[:, :], ident[:, :]).then_inc(adjT_psum, 1)
            pe.wait_ge(adjT_ready, 1)
            pe.wait_ge(ones_ready, 1)
            pe.matmul(psum[0:RANKS, 1, 0:P], ones[:, :], adjT[:, :], start=True, stop=True).then_inc(deg_psum, 1)
            pe.wait_ge(b_summed, 1)
            n = SKIPS * GATES
            pe.transpose(psum[:, 2, 0:n], b_sum[:, :], ident[0:n, 0:n]).then_inc(b_psum, 1)
            for p in range(SKIPS):
                pe.wait_ge(w_loaded[p % 2], 32 * (p // 2 + 1))
                for j in range(2):
                    if p >= 1:
                        pe.wait_ge(w_lo_ready, 2 * (p - 1) + j + 1)
                    for g in range(GATES):
                        mm = pe.transpose(psum[:, 4 + j, g * P:(g + 1) * P], w_raw[:, p % 2, j, g, :], ident[:, :])
                    mm.then_inc(w_psum, 1)

            pe.wait_ge(gnn_w_loaded, 16 * (3 + BT))
            pe.wait_ge(deg_ready, 1)
            pe.wait_ge(bias_rows_ready, 1)
            pe.wait_ge(wg1_ready, 1)
            pe.wait_ge(b_ready, 1)
            pe.wait_ge(w_lo_ready, 2 * SKIPS)
            with loop(pe, 0, gnn_iters) as it:
                for s in range(GNN_SLOTS):
                    pe.wait_ge(x_loaded[s], it * 16 + 16)
                    for b in range(BT):
                        mm = pe.matmul(psum[:, 2 * s, b * P:(b + 1) * P], x_tile[s][:, b, :], adjT[:, :], start=True, stop=True)
                    mm.then_inc(ax_psum, 1)
                for s in range(GNN_SLOTS):
                    out = psum[:, 2 * s + 1, :]
                    pe.wait_ge(h2_done, it * GNN_SLOTS + s + 1)
                    pe.matmul(out, deg_rows[:, 0, :], bg0_rows[:, :, :], start=True, stop=False, skip_group_check=True)
                    pe.wait_ge(axT_ready, it * GNN_SLOTS + s + 1)
                    for b in range(BT):
                        mm = pe.matmul(out[:, b * P:(b + 1) * P], axT[s][:, b * P:(b + 1) * P], wg0[:, :], start=False,
                                       stop=(b == BT - 1), skip_group_check=True)
                    mm.then_inc(h1_psum, 1)
                for s in range(GNN_SLOTS):
                    pe.wait_ge(h1_ready, it * GNN_SLOTS + s + 1)
                    for b in range(BT):
                        mm = pe.matmul(psum[:, 2 * s, b * P:(b + 1) * P], h1[s][:, b, :], adjT[:, :], start=True, stop=True)
                    mm.then_inc(ah_psum, 1)
                for s in range(GNN_SLOTS):
                    out = psum[:, 2 * s + 1, :]
                    pe.matmul(out, bg1_rows[:, :], deg_rows[:, :, :], start=True, stop=False)
                    pe.wait_ge(ahT_ready, it * GNN_SLOTS + s + 1)
                    cols = bass.ds(it * (GNN_SLOTS * TW) + s * TW, TW)
                    pe.matmul(out, wg1_hi[:, :], hT_hi[:, cols], start=False, stop=False)
                    pe.matmul(out, wg1_hi[:, :], hT_lo[:, cols], start=False, stop=False)
                    pe.matmul(out, wg1_lo[:, :], hT_hi[:, cols], start=False, stop=True).then_inc(h2_psum, 1)

            pe.wait_ge(h2_done, tiles + GNN_SLOTS)
            for ph in phases:
                with loop(pe, 0, ph.iters) as it:
                    for tile, t, k, forgets in ph.body():
                        n = it * ph.per_iter + (ph.items_before + k)
                        s = k % 2
                        order = (I, G, O) if t == 0 else (F, I, G, O)
                        pe.wait_ge(gates_read, n + (CREDIT - 1))
                        if t == 0 and ph.p > 1:
                            done = phases[ph.p - 2].items_for((tile + 1) * ph.batches)
                            pe.wait_ge(h_done, done + CREDIT)
                        xh, xl = windows_at(ph, hi_bt, it, tile, t), windows_at(ph, lo_bt, it, tile, t)
                        for g in order:
                            out = psum[:, 4 * s + g, 0:ph.width]
                            wh, wl = w_hi[:, ph.p - 1, 0, g, :], w_lo[:, ph.p - 1, 0, g, :]
                            pe.matmul(out, wh, xh, start=True, stop=False)
                            pe.matmul(out, wh, xl, start=False, stop=False)
                            mm = pe.matmul(out, wl, xh, start=False, stop=(t == 0))
                            if t == 0:
                                mm.then_inc(gate_psum[g], 1)
                        if t == 0:
                            continue
                        pe.wait_ge(h_done, n + (CREDIT - 1))
                        hh, hl = hs_hi[:, s, 0:ph.width], hs_lo[:, s, 0:ph.width]
                        for g in order:
                            out = psum[:, 4 * s + g, 0:ph.width]
                            wh, wl = w_hi[:, ph.p - 1, 1, g, :], w_lo[:, ph.p - 1, 1, g, :]
                            pe.matmul(out, wh, hh, start=False, stop=False)
                            pe.matmul(out, wh, hl, start=False, stop=False)
                            pe.matmul(out, wl, hh, start=False, stop=True).then_inc(gate_psum[g], 1)

        @block.scalar
        def _(act):
            for k in range(2 * SKIPS):
                p, j = k // 2, k % 2
                act.wait_ge(w_psum, k + 1)
                act.activation(w_hi[:, p, j], psum[:, 4 + j, :].rearrange("p (g h) -> p g h", g=GATES),
                               ACT.Copy).then_inc(w_hi_ready, 1)
            with loop(act, 0, gnn_iters) as it:
                for s in range(GNN_SLOTS):
                    act.wait_ge(ax_psum, it * GNN_SLOTS + s + 1)
                    act.activation(axT[s], psum[:, 2 * s, :], ACT.Copy).then_inc(axT_ready, 1)
                for s in range(GNN_SLOTS):
                    act.wait_ge(ah_psum, it * GNN_SLOTS + s + 1)
                    cols = bass.ds(it * (GNN_SLOTS * TW) + s * TW, TW)
                    act.activation(hT_hi[:, cols], psum[:, 2 * s, :], ACT.Copy).then_inc(ahT_hi, 1)
                for s in range(GNN_SLOTS):
                    act.wait_ge(h2_psum, it * GNN_SLOTS + s + 1)
                    cols = bass.ds((it * GNN_SLOTS + s) * TW, TW)
                    act.activation(hT_hi[:, cols], psum[:, 2 * s + 1, :], ACT.Relu).then_inc(h2_hi, 1)

            act.wait_ge(b_ready, 1)
            act.wait_ge(h1_ready, tiles)
            for ph in phases:
                with loop(act, 0, ph.iters) as it:
                    def tanh_of(k):
                        n = it * ph.per_iter + (ph.items_before + k)
                        act.wait_ge(c_ready, n + 1)
                        act.activation(tanh_c[k % 2][:, 0:ph.width], cell[k % 2][:, 0:ph.width], ACT.Tanh).then_inc(tanh_ready, 1)

                    pending = None
                    for tile, t, k, forgets in ph.body():
                        n = it * ph.per_iter + (ph.items_before + k)
                        nf = it * ph.f_per_iter + (ph.f_before + forgets)
                        s = k % 2
                        for g in ((I, G, O) if t == 0 else (F, I, G, O)):
                            act.wait_ge(gate_psum[g], nf if g == F else n + 1)
                            if g == O:
                                act.wait_ge(h_mul, n + (CREDIT - 1))
                            b = (ph.p - 1) * GATES + g
                            op = act.activation(gate[s][g][:, 0:ph.width], psum[:, 4 * s + g, 0:ph.width],
                                                ACT.Tanh if g == G else ACT.Sigmoid, bias=bias[:, b:b + 1])
                            if g == F:
                                op.then_inc(f_ready, 1)
                            elif g == G:
                                op.then_inc(ig_ready, 1)
                            elif g == O:
                                op.then_inc(gates_read, 1)
                            if pending is not None:
                                tanh_of(pending)
                                pending = None
                        if k + 1 < ph.per_iter and (k + 1) % (2 * ph.p) < 2:
                            pending = k
                        else:
                            tanh_of(k)

        @block.vector
        def _(dve):
            dve.memset(ones[:, :], 1.0).then_inc(ones_ready, 1)
            dve.memset(bg0_rows[:, :, :].bitcast(F32), 0.0)
            dve.memset(bg1_rows[:, :].bitcast(F32), 0.0).then_inc(ones_ready, 1)
            dve.wait_ge(ones_ready, 2)
            dve.memset(start[:, 0:1], 0.0).then_inc(h2_done, GNN_SLOTS)
            dve.memset(start[:, 1:2], 0.0).then_inc(gates_read, CREDIT)
            dve.memset(start[:, 2:3], 0.0).then_inc(h_done, CREDIT)
            dve.memset(start[:, 3:4], 0.0).then_inc(h_mul, CREDIT)
            dve.wait_ge(adjT_psum, 1)
            dve.tensor_copy(adjT[:, :], psum[:, 0, 0:P]).then_inc(adjT_ready, 1)
            dve.wait_ge(b_loaded, 32)
            dve.tensor_tensor(b_sum[:, :], b_raw[:, 0, :], b_raw[:, 1, :], ALU.add).then_inc(b_summed, 1)
            dve.wait_ge(deg_psum, 1)
            for b in range(BT):
                op = dve.tensor_copy(deg_rows[:, b, :], psum[0:RANKS, 1, 0:P])
            op.then_inc(deg_hi, 1)
            dve.wait_ge(deg_hi, 1)
            lo = slice(DEG_LO, DEG_LO + 1)
            for b in range(BT):
                op = dve.tensor_tensor(deg_rows[lo, b, :], psum[lo, 1, 0:P], deg_rows[lo, b, :].bitcast(F32), ALU.subtract)
            op.then_inc(deg_ready, 1)
            dve.wait_ge(gnn_w_loaded, 16 * (3 + BT))
            for rows, raw in ((bg0_rows, bg0_raw), (bg1_rows, bg1_raw)):
                for at in (0, DEG_LO, BIAS_LO):
                    op = dve.tensor_copy(rows[at:at + 1], raw[at:at + 1])
            op.then_inc(bias_hi, 1)
            dve.wait_ge(bias_hi, 1)
            lo = slice(BIAS_LO, BIAS_LO + 1)
            for rows, raw in ((bg0_rows, bg0_raw), (bg1_rows, bg1_raw)):
                op = dve.tensor_tensor(rows[lo], raw[lo], rows[lo].bitcast(F32), ALU.subtract)
            op.then_inc(bias_rows_ready, 1)
            dve.tensor_copy(wg1_hi[:, :], wg1).then_inc(wg1_cut, 1)
            dve.wait_ge(wg1_cut, 1)
            dve.tensor_tensor(wg1_lo[:, :], wg1, wg1_hi[:, :].bitcast(F32), ALU.subtract).then_inc(wg1_ready, 1)
            dve.wait_ge(b_psum, 1)
            dve.tensor_copy(bias[:, :], psum[:, 2, 0:SKIPS * GATES]).then_inc(b_ready, 1)
            for k in range(2 * SKIPS):
                p, j = k // 2, k % 2
                dve.wait_ge(w_hi_ready, k + 1)
                dve.tensor_tensor(w_lo[:, p, j], psum[:, 4 + j, :].rearrange("p (g h) -> p g h", g=GATES),
                                  w_hi[:, p, j].bitcast(F32), ALU.subtract).then_inc(w_lo_ready, 1)
            with loop(dve, 0, gnn_iters) as it:
                for s in range(GNN_SLOTS):
                    dve.wait_ge(h1_psum, it * GNN_SLOTS + s + 1)
                    dve.tensor_scalar(h1[s], psum[:, 2 * s + 1, :].rearrange("p (b h) -> p b h", b=BT), 0.0, None,
                                      ALU.max).then_inc(h1_ready, 1)
                for s in range(GNN_SLOTS):
                    dve.wait_ge(ahT_hi, it * GNN_SLOTS + s + 1)
                    cols = bass.ds(it * (GNN_SLOTS * TW) + s * TW, TW)
                    dve.tensor_tensor(hT_lo[:, cols], psum[:, 2 * s, :], hT_hi[:, cols].bitcast(F32),
                                      ALU.subtract).then_inc(ahT_ready, 1)
                for s in range(GNN_SLOTS):
                    dve.wait_ge(h2_hi, it * GNN_SLOTS + s + 1)
                    cols = bass.ds(it * (GNN_SLOTS * TW) + s * TW, TW)
                    dve.scalar_tensor_tensor(out=hT_lo[:, cols], in0=psum[:, 2 * s + 1, :], scalar=0.0,
                                             in1=hT_hi[:, cols].bitcast(F32), op0=ALU.max,
                                             op1=ALU.subtract).then_inc(h2_done, 1)

            for ph in phases:
                with loop(dve, 0, ph.iters) as it:
                    def place(tile, t, k):
                        if t == ph.p - 1:
                            return (windows_at(ph, hi_bt, it, tile, t), windows_at(ph, lo_bt, it, tile, t),
                                    as_windows(ph, h_full[k % 2][:, 0:ph.width]))
                        return hs_hi[:, k % 2, 0:ph.width], hs_lo[:, k % 2, 0:ph.width], h_full[k % 2][:, 0:ph.width]

                    def split(tile, t, k):
                        n = it * ph.per_iter + (ph.items_before + k)
                        hi, lo, full = place(tile, t, k)
                        dve.wait_ge(h_mul, n + (CREDIT + 1))
                        dve.tensor_copy(hi, full).then_inc(h_hi, 1)
                        dve.wait_ge(h_hi, n + 1)
                        dve.tensor_tensor(lo, full, hi.bitcast(F32), ALU.subtract).then_inc(h_done, 1)

                    before = None
                    for tile, t, k, forgets in ph.body():
                        n = it * ph.per_iter + (ph.items_before + k)
                        nf = it * ph.f_per_iter + (ph.f_before + forgets)
                        s = k % 2
                        c = cell[s][:, 0:ph.width]
                        if t > 0:
                            dve.wait_ge(f_ready, nf)
                            dve.tensor_tensor(c, c, gate[s][F][:, 0:ph.width], ALU.mult).then_inc(fc_done, 1)
                        dve.wait_ge(ig_ready, n + 1)
                        i_g = c if t == 0 else in_gate[:, 0:ph.width]
                        op = dve.tensor_tensor(i_g, gate[s][I][:, 0:ph.width], gate[s][G][:, 0:ph.width], ALU.mult)
                        if t == 0:
                            op.then_inc(c_ready, 1)
                        else:
                            op.then_inc(ig_done, 1)
                            dve.wait_ge(fc_done, nf)
                            dve.wait_ge(ig_done, nf)
                            dve.tensor_tensor(c, c, i_g, ALU.add).then_inc(c_ready, 1)
                        if before:
                            split(*before)
                            before = None
                        dve.wait_ge(tanh_ready, n + 1)
                        dve.tensor_tensor(h_full[s][:, 0:ph.width], gate[s][O][:, 0:ph.width], tanh_c[s][:, 0:ph.width],
                                          ALU.mult).then_inc(h_mul, 1)
                        if t == ph.p - 1:
                            before = (tile, t, k)
                        else:
                            split(tile, t, k)
                    if before:
                        split(*before)


def back(nc, hT_hi, hT_lo, ident, adj_sb, psum, x, W_lin, W_val, a, W_out, src, dst, out):
    B = x.shape[0]
    tiles = B // BT
    TW = BT * P
    HEADS, DH = a.shape
    E = src.shape[0]
    EC = E // P
    GROUP = P // HEADS
    groups = B // GROUP
    pairs = GROUP // BT // 2
    GT = 2 * pairs
    KEPT = 2 * pairs + 1
    kept_from = [(1 + g * pairs) % KEPT for g in range(groups)]
    assert all(first + pairs <= KEPT for first in kept_from)
    phases = [("edges", 0)]
    for g in range(1, groups):
        phases += [("edges", g), ("mix", g - 1)]
    phases += [("mix", groups - 1)]

    with ExitStack() as ctx:
        def sb(name, shape, dt=F32):
            return ctx.enter_context(nc.sbuf_tensor(name, shape, dt))

        def sem(name):
            return ctx.enter_context(nc.semaphore(name))

        x1_kept = sb("x1_kept", [P, KEPT * 2 * BT, P])
        room = sb("room", [P, 2 * EC * TW + 2 * TW])
        space, taken = [x1_kept[:, :, :].rearrange("p b d -> p (b d)")], [0]

        def part(width):
            taken[0] += width
            return space[0][:, taken[0] - width:taken[0]]

        edge_row_i = part(2 * E).bitcast(I32).rearrange("p (j e) -> p j e", j=2)
        edge_col_i = sb("edge_col_i", [P, 2, EC], I32)
        edge_row = part(2 * E).rearrange("p (j e) -> p j e", j=2)
        edge_col = sb("edge_col", [P, EC, 2])
        count_i = part(E).bitcast(I32)
        count = part(E)
        index_i = sb("index_i", [P, EC], I32)
        index = sb("index", [P, EC])
        key_row = part(E)
        key_col = sb("key_col", [P, EC])
        less = part(E)
        rank = sb("rank", [P, EC])
        permute = part(EC * E).rearrange("p (c e) -> p c e", c=EC)
        spread = part(2 * EC * P).rearrange("p (j c n) -> p j c n", j=2, c=EC)
        sorted_row = part(2 * E).rearrange("p (j e) -> p j e", j=2)
        sorted_col = sb("sorted_col", [P, EC, 2])
        at_node = part(2 * E).rearrange("p (j e) -> p j e", j=2)
        to_r = sb("to_r", [P, E], F32R)
        ends = sb("ends", [P, E], F32R)
        from_node = sb("from_node", [P, EC, P])
        to_node = part(EC * P).rearrange("p (c n) -> p c n", c=EC)
        adj_edge = sb("adj_edge", [P, EC])
        log_adj = sb("log_adj", [P, EC])
        log_diag = part(EC * P).rearrange("p (c e) -> p c e", c=EC)
        log_row = sb("log_row", [P, E])
        same_f, same_b = sb("same_f", [P, E]), part(E)
        cap_f, cap_b = sb("cap_f", [P, E]), sb("cap_b", [P, E])
        ones = sb("ones2", [P, P])
        minus_half = sb("minus_half", [P, BT])
        eps = sb("eps", [P, BT])
        zero = sb("zero", [P, BT])
        START = 12
        start = sb("start2", [P, START])
        w_nat = part(3 * P).rearrange("p (j d) -> p j d", j=3)
        w_qv = sb("w_qv", [P, 2 * P])
        w_outT = sb("w_outT", [P, P])
        PAIR_ROWS = 2 * BT * HEADS
        A_COL = PAIR_ROWS - HEADS
        a_wide = sb("a_wide", [P, A_COL + P])

        space[0], taken[0] = room, 0
        hsum = part(2 * TW).rearrange("p (s b t) -> p s b t", s=2, b=BT)
        leaky = part(4 * E).rearrange("p (h b e) -> p h b e", h=2, b=2)
        row_b, row_c, row_d = (part(E) for n in "bcd")
        xq_hi = sb("xq_hi", [P, 2, 2, P], F32R)
        xq_lo = sb("xq_lo", [P, 2, 2, P], F32R)
        x_res = sb("x_res", [P, 2, BT, P])
        y = sb("y", [P, 2, BT, P])
        stats = sb("stats", [P, 2, BT, 6])
        moments = sb("moments", [P, 2, BT, 2])
        var_eps = sb("var_eps", [P, 2, BT])
        rstd = sb("rstd", [P, 2, BT])
        minus_mean = sb("minus_mean", [P, 2, BT])
        shift = sb("shift", [P, 2, BT])
        taken[0] = 0
        va = part(2 * EC * TW).rearrange("p (s c w) -> p s c w", s=2, c=EC)
        yT = part(2 * TW).rearrange("p (s w) -> p s w", s=2)
        x1T = sb("x1T", [P, 2, TW])
        row_a = sb("row_a", [P, E])
        attn = sb("attn", [P, EC, P])
        rows = sb("rows", [P, E])

        names = ("ones_done rows_loaded cols_loaded w_loaded a_loaded iota_done a_zero tables_f ranks permutes spreads rows_psum "
                 "rows_ready onehots adj_psum adj_done eps_done log_done diag_done log_psum log_ready sames shifted caps wT_psum wT_ready "
                 "key_done ecol_done "
                 "hsum_ready t_psum y_done stats_done moments_done var_done rstd_done shift_done x1_done x1_kept_ready xt_psum xT_ready "
                 "qv_psum xq_ready hi_ready xv_ready z_psum slope_ready leaky_ready edges_psum "
                 "row_copied log_added max_f max_b below_max exp_done sum_f sum_b recip_done attn_row attn_psum attn_ready "
                 "vg_psum va_ready yt_psum yT_ready o_psum o_read stats2_done moments2_done var2_done rstd2_done shift2_done out_ready")
        S = {n: sem("b_" + n) for n in names.split()}
        x_loaded = [sem(f"b_x_loaded{s}") for s in range(2)]
        stored = [sem(f"b_stored{s}") for s in range(2)]
        CREDIT = 2

        T_BANK, QV_BANK, Z_BANK, SCORE_BANK = 0, 2, 4, 6
        VG_BANK, YT_BANK, O_BANK = 0, 4, 6
        ATTN_BANK = Z_BANK
        SUB = ALU.subtract

        block = ctx.enter_context(nc.Block())

        def bank2(b):
            return psum[:, b:b + 2, :]

        hi_t = hT_hi[:, :].rearrange("p (b d) -> p b d", d=P)
        lo_t = hT_lo[:, :].rearrange("p (b d) -> p b d", d=P)

        score_banks = psum[:, SCORE_BANK:SCORE_BANK + 2, :].rearrange("p k c -> p (k c)")

        def tile_of(g, j, s):
            return g * GT + s + 2 * j

        def steps(engine, last):
            with loop(engine, 0, pairs - 1) as j:
                yield j, False
            yield pairs - 1, last


        @block.sync
        def _(sp):
            for s in range(2):
                sp.dma_start(x_res[:, s], x[s * BT:(s + 1) * BT].rearrange("b t d -> t b d")).then_inc(x_loaded[s], 16)
            with loop(sp, 0, tiles // 2 - 1) as it:
                for s in range(2):
                    sp.wait_ge(S["y_done"], 2 * it + s + 1)
                    sp.dma_start(x_res[:, s], x[bass.ds((2 * it + 2 + s) * BT, BT)].rearrange("b t d -> t b d")).then_inc(x_loaded[s], 16)

        @block.gpsimd
        def _(pool):
            for j, e in enumerate((src, dst)):
                pool.dma_start(edge_row_i[:, j, :], e.rearrange("(a e) -> a e", a=1).broadcast_to([P, E])).then_inc(S["rows_loaded"], 16)
                pool.dma_start(edge_col_i[:, j, :], e.rearrange("(c p) -> p c", p=P), allow_slow_non_contiguous=True).then_inc(S["cols_loaded"], 16)
            for j, w in enumerate((W_lin, W_val, W_out)):
                pool.dma_start(w_nat[:, j, :], w).then_inc(S["w_loaded"], 16)
            pool.memset(a_wide[:, :], 0.0).then_inc(S["a_zero"], 1)
            pool.iota(count_i[:, :], pattern=[[1, E]], base=0, channel_multiplier=0).then_inc(S["iota_done"], 1)
            pool.iota(index_i[:, :], pattern=[[P, EC]], base=0, channel_multiplier=1).then_inc(S["iota_done"], 1)
            pool.wait_ge(S["a_zero"], 1)
            for h in range(HEADS):
                pool.dma_start(a_wide[h * DH:(h + 1) * DH, A_COL + h:A_COL + h + 1], a[h].rearrange("(d o) -> d o", o=1), allow_slow_non_contiguous=True).then_inc(S["a_loaded"], 16)


            def norm_factors(s, ready, var_sem, rstd_sem, shift_sem, k, credit=0):
                pool.wait_ge(ready, k + 1)
                if credit:
                    pool.wait_ge(S["out_ready"], k + (credit - 1))
                pool.tensor_tensor(minus_mean[:, s, :], zero[:, :], moments[:, s, :, 0], SUB)
                pool.tensor_tensor(var_eps[:, s, :], moments[:, s, :, 1], eps[:, :], ALU.add).then_inc(var_sem, 1)
                pool.wait_ge(var_sem, k + 1)
                pool.tensor_tensor(rstd[:, s, :], var_eps[:, s, :], minus_half[:, :], ALU.pow).then_inc(rstd_sem, 1)
                pool.wait_ge(rstd_sem, k + (credit + 1))
                pool.tensor_tensor(shift[:, s, :], minus_mean[:, s, :], rstd[:, s, :], ALU.mult).then_inc(shift_sem, 1)

            def layer_norm_ahead(k):
                for s in range(2):
                    pool.wait_ge(S["t_psum"], k + s + 1)
                    cols = bass.ds((k + s) * TW, TW)
                    pool.tensor_tensor(hsum[:, s].rearrange("p b t -> p (b t)"), hT_hi[:, cols].bitcast(F32),
                                       hT_lo[:, cols].bitcast(F32), ALU.add).then_inc(S["hsum_ready"], 1)
                for s in range(2):
                    norm_factors(s, S["moments_done"], S["var_done"], S["rstd_done"], S["shift_done"], k + s)

            pool.wait_ge(S["diag_done"], EC)
            layer_norm_ahead(0)
            for phase, g in phases:
                with loop(pool, 0, pairs - (phase == "edges" and g == groups - 1)) as j:
                    if phase == "edges":
                        layer_norm_ahead(tile_of(g, j, 2))
                    else:
                        for s in range(2):
                            norm_factors(s, S["moments2_done"], S["var2_done"], S["rstd2_done"], S["shift2_done"], tile_of(g, j, s), CREDIT)

        @block.tensor
        def _(pe):
            pe.wait_ge(S["w_loaded"], 48)
            for j in range(3):
                mm = pe.transpose(psum[:, 0, j * P:(j + 1) * P], w_nat[:, j, :], ident[:, :])
            mm.then_inc(S["wT_psum"], 1)
            pe.wait_ge(S["permutes"], EC)
            pe.wait_ge(S["spreads"], 2 * EC)
            for j in range(2):
                for c in range(EC):
                    pe.matmul(psum[:, 2, j * E:(j + 1) * E], spread[:, j, c, :], permute[:, c, :], start=(c == 0), stop=(c == EC - 1))
            for r in range(EC):
                for c in range(EC):
                    mm = pe.matmul(psum[:, 3, 2 * r:2 * r + 2], permute[:, c, r * P:(r + 1) * P], edge_col[:, c, :],
                                   start=(c == 0), stop=(c == EC - 1))
            mm.then_inc(S["rows_psum"], 1)
            pe.wait_ge(S["onehots"], 2)
            for c in range(EC):
                mm = pe.matmul(psum[:, 4, c * P:(c + 1) * P], at_node[:, 0, c * P:(c + 1) * P], adj_sb[:, :], start=True, stop=True)
            mm.then_inc(S["adj_psum"], 1)
            pe.wait_ge(S["diag_done"], EC)
            for c in range(EC):
                mm = pe.matmul(psum[:, 5, c * P:(c + 1) * P], ones[:, :], log_diag[:, c, :], start=True, stop=True)
            mm.then_inc(S["log_psum"], 1)
            pe.wait_ge(S["wT_ready"], 2)
            pe.wait_ge(S["caps"], 2)
            pe.wait_ge(S["log_ready"], 1)
            pe.wait_ge(S["a_loaded"], 16 * HEADS)

            def turn_h(k, s):
                pe.wait_ge(S["hsum_ready"], k + 1)
                for b in range(BT):
                    mm = pe.transpose(psum[:, T_BANK + s, b * P:(b + 1) * P], hsum[:, s, b, :], ident[:, :])
                mm.then_inc(S["t_psum"], 1)

            def turn_x1(k, s):
                pe.wait_ge(S["x1_done"], k + 1)
                for b in range(BT):
                    mm = pe.transpose(psum[:, T_BANK + s, b * P:(b + 1) * P], y[:, s, b, :], ident[:, :])
                mm.then_inc(S["xt_psum"], 1)

            def project(k, s, h):
                pe.wait_ge(S["xT_ready"], k + 1)
                pe.wait_ge(S["xv_ready"], 2 * k + (h + 1))
                for b in range(2):
                    mm = pe.matmul(psum[:, QV_BANK + h, b * 2 * P:(b + 1) * 2 * P], x1T[:, s, (2 * h + b) * P:(2 * h + b + 1) * P],
                                   w_qv[:, :], start=True, stop=True)
                mm.then_inc(S["qv_psum"], 1)

            def gather(k, h):
                pe.wait_ge(S["xq_ready"], 2 * k + (h + 1))
                for b in range(2):
                    z = psum[:, Z_BANK + h, b * E:(b + 1) * E]
                    pe.matmul(z, xq_hi[:, h, b, :], ends[:, :], start=True, stop=False)
                    mm = pe.matmul(z, xq_lo[:, h, b, :], ends[:, :], start=False, stop=True)
                mm.then_inc(S["z_psum"], 1)

            def edge_scores(g, k, j, s, h):
                pe.wait_ge(S["leaky_ready"], 2 * k + (h + 1))
                if s == 0 and h == 0 and g > 0:
                    pe.wait_ge(S["row_copied"], g)
                for b in range(2):
                    n = s * BT + 2 * h + b
                    mm = pe.matmul(score_banks[:, bass.ds(j * E, E)], a_wide[:, A_COL - n * HEADS:A_COL - n * HEADS + P],
                                   leaky[:, h, b, :], start=(n == 0), stop=(n == 2 * BT - 1), skip_group_check=True)
                return mm

            def edge_pair(g, j, last):
                k, ahead = tile_of(g, j, 0), tile_of(g, j, 2)
                pe.wait_ge(S["xT_ready"], k + 1)
                if not last:
                    turn_h(ahead, 0)
                project(k, 0, 0)
                project(k, 0, 1)
                if not last:
                    pe.wait_ge(S["xT_ready"], k + 2)
                    turn_h(ahead + 1, 1)
                gather(k, 0)
                project(k + 1, 1, 0)
                gather(k, 1)
                edge_scores(g, k, j, 0, 0)
                project(k + 1, 1, 1)
                gather(k + 1, 0)
                edge_scores(g, k, j, 0, 1)
                gather(k + 1, 1)
                edge_scores(g, k + 1, j, 1, 0)
                if not last:
                    turn_x1(ahead, 0)
                edge_scores(g, k + 1, j, 1, 1).then_inc(S["edges_psum"], 1)
                if not last:
                    turn_x1(ahead + 1, 1)

            def attention_by_edge(g):
                pe.wait_ge(S["attn_row"], g + 1)
                for c in range(EC):
                    mm = pe.transpose(psum[:, ATTN_BANK, c * P:(c + 1) * P], row_a[:, c * P:(c + 1) * P], ident[:, :])
                mm.then_inc(S["attn_psum"], 1)

            def value_gather(k, j, s):
                for c in range(EC):
                    out_c = psum[:, VG_BANK + 2 * s + c, :]
                    to = to_r[:, c * P:(c + 1) * P]
                    pe.matmul(out_c, to, hi_t[:, bass.ds(k * BT, BT), :], start=True, stop=False)
                    mm = pe.matmul(out_c, to, lo_t[:, bass.ds(k * BT, BT), :], start=False, stop=True)
                mm.then_inc(S["vg_psum"], 1)

            def sum_by_source(k, s):
                pe.wait_ge(S["va_ready"], k + 1)
                for b in range(BT):
                    for c in range(EC):
                        mm = pe.matmul(psum[:, YT_BANK + s, b * P:(b + 1) * P], va[:, s, c, b * P:(b + 1) * P],
                                       from_node[:, c, :], start=(c == 0), stop=(c == EC - 1))
                mm.then_inc(S["yt_psum"], 1)

            def output(k, s):
                pe.wait_ge(S["yT_ready"], k + 1)
                pe.wait_ge(S["o_read"], k + 1)
                for b in range(BT):
                    mm = pe.matmul(psum[:, O_BANK + s, b * P:(b + 1) * P], yT[:, s, b * P:(b + 1) * P], w_outT[:, :],
                                   start=True, stop=True)
                mm.then_inc(S["o_psum"], 1)

            def mix_pair(g, j, last):
                k = tile_of(g, j, 0)
                for s in range(2):
                    sum_by_source(k + s, s)
                if not last:
                    for s in range(2):
                        value_gather(tile_of(g, j, 2 + s), j, s)
                for s in range(2):
                    output(k + s, s)

            for s in range(2):
                turn_h(s, s)
            for s in range(2):
                turn_x1(s, s)
            mixed = 0
            for phase, g in phases:
                if phase == "edges":
                    pe.wait_ge(S["o_read"], mixed * GT + CREDIT)
                    for j, last in steps(pe, g == groups - 1):
                        edge_pair(g, j, last)
                    if g > 0:
                        attention_by_edge(g - 1)
                        pe.wait_ge(S["attn_ready"], g)
                else:
                    if g == groups - 1:
                        attention_by_edge(g)
                        pe.wait_ge(S["attn_ready"], g + 1)
                    started = min(g + 2, groups)
                    pe.wait_ge(S["xT_ready"], min(started * GT + 2, tiles))
                    pe.wait_ge(S["xv_ready"], 2 * started * GT + CREDIT)
                    pe.wait_ge(S["row_copied"], started)
                    for s in range(2):
                        value_gather(tile_of(g, 0, s), 0, s)
                    for j, last in steps(pe, True):
                        mix_pair(g, j, last)
                    mixed += 1

        @block.scalar
        def _(act):
            act.wait_ge(S["eps_done"], 1)
            act.activation(log_adj[:, :], adj_edge[:, :], ACT.Ln).then_inc(S["log_done"], 1)

            def half_bank(h):
                return psum[:, QV_BANK + h, :].rearrange("p (b w) -> p b w", b=2)

            def query_and_value(k, h):
                act.wait_ge(S["qv_psum"], 2 * k + (h + 1))
                act.activation(xq_hi[:, h], half_bank(h)[:, :, 0:P], ACT.Copy)
                act.activation(hi_t[:, bass.ds(k * BT + 2 * h, 2), :], half_bank(h)[:, :, P:2 * P], ACT.Copy).then_inc(S["hi_ready"], 1)

            def slope_times(k, h):
                act.wait_ge(S["z_psum"], 2 * k + (h + 1))
                act.activation(leaky[:, h], psum[:, Z_BANK + h, :].rearrange("p (b e) -> p b e", b=2), ACT.Copy,
                               scale=SLOPE).then_inc(S["slope_ready"], 1)

            def normalize(s, row_of, shift_sem, done_sem, n):
                act.wait_ge(shift_sem, n + 1)
                for b in range(BT):
                    op = act.activation(row_of(b), row_of(b), ACT.Identity, bias=shift[:, s, b:b + 1], scale=rstd[:, s, b:b + 1])
                op.then_inc(done_sem, 1)

            def normalize_x1(k, s):
                normalize(s, lambda b: y[:, s, b, :], S["shift_done"], S["x1_done"], k)

            def x1_turned(k, s):
                act.wait_ge(S["xt_psum"], k + 1)
                act.activation(x1T[:, s, :], psum[:, T_BANK + s, :], ACT.Copy).then_inc(S["xT_ready"], 1)

            def copy_yT(g, j):
                for s in range(2):
                    act.wait_ge(S["yt_psum"], tile_of(g, j, s) + 1)
                    act.activation(yT[:, s, :], psum[:, YT_BANK + s, :], ACT.Copy).then_inc(S["yT_ready"], 1)

            def normalize_and_store(g, j):
                for s in range(2):
                    k = tile_of(g, j, s)
                    first = kept_from[g] * 2 * BT + s * BT
                    normalize(s, lambda b: x1_kept[:, bass.ds(j * (2 * BT) + (first + b), 1), :].rearrange("p o d -> p (o d)"),
                              S["shift2_done"], S["out_ready"], k)
                for s in range(2):
                    k = tile_of(g, j, s)
                    first = kept_from[g] * 2 * BT + s * BT
                    act.wait_ge(S["out_ready"], k + (CREDIT + 1))
                    act.dma_start(out[bass.ds(k * BT, BT)].rearrange("b t d -> t b d"),
                                  x1_kept[:, bass.ds(j * (2 * BT) + first, BT), :]).then_inc(stored[s], 16)

            for s in range(2):
                normalize_x1(s, s)
            for s in range(2):
                x1_turned(s, s)
            for phase, g in phases:
                if phase == "edges":
                    if g > 0:
                        act.wait_ge(S["below_max"], g)
                        act.activation(row_d[:, :], row_c[:, :], ACT.Exp).then_inc(S["exp_done"], 1)
                    for j, last in steps(act, g == groups - 1):
                        k = tile_of(g, j, 0)
                        query_and_value(k, 0)
                        query_and_value(k, 1)
                        slope_times(k, 0)
                        query_and_value(k + 1, 0)
                        slope_times(k, 1)
                        query_and_value(k + 1, 1)
                        slope_times(k + 1, 0)
                        if not last:
                            normalize_x1(tile_of(g, j, 2), 0)
                        slope_times(k + 1, 1)
                        if not last:
                            normalize_x1(tile_of(g, j, 3), 1)
                        if not last:
                            for s in range(2):
                                x1_turned(tile_of(g, j, 2 + s), s)
                    act.wait_ge(S["edges_psum"], (g + 1) * pairs)
                    for j in range(pairs):
                        op = act.activation(rows[j * PAIR_ROWS:(j + 1) * PAIR_ROWS, :], score_banks[0:PAIR_ROWS, j * E:(j + 1) * E], ACT.Copy)
                    op.then_inc(S["row_copied"], 1)
                    if g == groups - 1:
                        act.wait_ge(S["below_max"], g + 1)
                        act.activation(row_d[:, :], row_c[:, :], ACT.Exp).then_inc(S["exp_done"], 1)
                else:
                    copy_yT(g, 0)
                    for j, last in steps(act, True):
                        if not last:
                            copy_yT(g, j + 1)
                        normalize_and_store(g, j)
            for s in range(2):
                act.wait_ge(stored[s], 16 * (tiles // 2))

        @block.vector
        def _(dve):
            dve.memset(ones[:, :], 1.0).then_inc(S["ones_done"], 1)
            dve.memset(minus_half[:, :], -0.5).then_inc(S["ones_done"], 1)
            dve.memset(eps[:, :], LN_EPS).then_inc(S["ones_done"], 1)
            dve.memset(zero[:, :], 0.0).then_inc(S["ones_done"], 1)
            for n, freed in enumerate((S["t_psum"], S["x1_kept_ready"], S["xv_ready"], S["o_read"], S["out_ready"], S["rstd2_done"])):
                dve.memset(start[:, n:n + 1], 0.0).then_inc(freed, CREDIT)

            dve.wait_ge(S["wT_psum"], 1)
            dve.tensor_copy(w_qv[:, :], psum[:, 0, 0:2 * P]).then_inc(S["wT_ready"], 1)
            dve.tensor_copy(w_outT[:, :], psum[:, 0, 2 * P:3 * P]).then_inc(S["wT_ready"], 1)

            dve.wait_ge(S["rows_loaded"], 32)
            dve.tensor_copy(edge_row, edge_row_i).then_inc(S["tables_f"], 1)
            dve.wait_ge(S["cols_loaded"], 32)
            for j in range(2):
                dve.tensor_copy(edge_col[:, :, j], edge_col_i[:, j, :]).then_inc(S["ecol_done"], 1)
            dve.wait_ge(S["iota_done"], 2)
            dve.tensor_copy(count[:, :], count_i[:, :]).then_inc(S["tables_f"], 1)
            dve.tensor_copy(index[:, :], index_i[:, :]).then_inc(S["tables_f"], 1)
            dve.wait_ge(S["tables_f"], 3)
            dve.wait_ge(S["ecol_done"], 2)
            dve.scalar_tensor_tensor(out=key_row[:, :], in0=edge_row[:, 0, :], scalar=float(E), in1=count[:, :],
                                     op0=ALU.mult, op1=ALU.add).then_inc(S["key_done"], 1)
            dve.scalar_tensor_tensor(out=key_col[:, :], in0=edge_col[:, :, 0], scalar=float(E), in1=index[:, :],
                                     op0=ALU.mult, op1=ALU.add).then_inc(S["key_done"], 1)
            for c in range(EC):
                for j in range(2):
                    dve.tensor_scalar(spread[:, j, c, :], ones[:, :], edge_col[:, c, j:j + 1], None, ALU.mult).then_inc(S["spreads"], 1)
            dve.wait_ge(S["key_done"], 2)
            for c in range(EC):
                if c:
                    dve.wait_ge(S["ranks"], c)
                dve.tensor_scalar(less[:, :], key_row[:, :], key_col[:, c:c + 1], 0.0, ALU.is_lt, ALU.add,
                                  accum_out=rank[:, c:c + 1]).then_inc(S["ranks"], 1)
            dve.wait_ge(S["ranks"], EC)
            for c in range(EC):
                dve.tensor_scalar(permute[:, c, :], count[:, :], rank[:, c:c + 1], None, ALU.is_equal).then_inc(S["permutes"], 1)
            dve.wait_ge(S["rows_psum"], 1)
            dve.tensor_copy(sorted_row, psum[:, 2, :].rearrange("p (j e) -> p j e", j=2)).then_inc(S["rows_ready"], 1)
            dve.tensor_copy(sorted_col[:, :, :], psum[:, 3, 0:2 * EC].rearrange("p (c j) -> p c j", j=2)).then_inc(S["rows_ready"], 1)
            dve.memset(same_f[:, 0:1], 0.0)
            dve.memset(same_b[:, E - 1:E], 0.0).then_inc(S["rows_ready"], 1)
            dve.wait_ge(S["rows_ready"], 3)
            for j in range(2):
                dve.tensor_scalar(at_node[:, j, :], sorted_row[:, j, :], index[:, 0:1], None, ALU.is_equal).then_inc(S["onehots"], 1)
            for j, of_edge in enumerate((from_node, to_node)):
                for c in range(EC):
                    op = dve.tensor_scalar(of_edge[:, c, :], count[:, 0:P], sorted_col[:, c, j:j + 1], None, ALU.is_equal)
            op.then_inc(S["onehots"], 1)
            dve.wait_ge(S["onehots"], 3)
            dve.tensor_copy(to_r[:, :], at_node[:, 1, :])
            dve.tensor_tensor(ends[:, :], at_node[:, 0, :], at_node[:, 1, :], ALU.add)
            dve.tensor_tensor(same_f[:, 1:E], sorted_row[:, 0, 1:E], sorted_row[:, 0, 0:E - 1], ALU.is_equal)
            dve.tensor_tensor(same_b[:, 0:E - 1], sorted_row[:, 0, 1:E], sorted_row[:, 0, 0:E - 1], ALU.is_equal).then_inc(S["sames"], 1)
            dve.wait_ge(S["sames"], 1)
            for same, cap in ((same_f, row_a), (same_b, row_b)):
                dve.tensor_scalar(cap[:, :], same[:, :], 2.0, -1.0, ALU.mult, ALU.add).then_inc(S["shifted"], 1)
            dve.wait_ge(S["shifted"], 2)
            for sign, cap in ((row_a, cap_f), (row_b, cap_b)):
                dve.tensor_scalar(cap[:, :], sign[:, :], FLT_MAX, None, ALU.mult).then_inc(S["caps"], 1)
            dve.wait_ge(S["adj_psum"], 1)
            for c in range(EC):
                if c:
                    dve.wait_ge(S["adj_done"], c)
                dve.tensor_tensor_reduce(less[:, 0:P], psum[:, 4, c * P:(c + 1) * P], to_node[:, c, :], 1.0, 0.0,
                                         ALU.mult, ALU.add, rank[:, c:c + 1]).then_inc(S["adj_done"], 1)
            dve.wait_ge(S["adj_done"], EC)
            dve.tensor_scalar(adj_edge[:, :], rank[:, :], LOG_EPS, None, ALU.add).then_inc(S["eps_done"], 1)
            dve.wait_ge(S["log_done"], 1)
            for c in range(EC):
                dve.tensor_scalar(log_diag[:, c, :], ident[:, :], log_adj[:, c:c + 1], None, ALU.mult).then_inc(S["diag_done"], 1)
            dve.wait_ge(S["log_psum"], 1)
            dve.tensor_copy(log_row[:, :], psum[:, 5, 0:E]).then_inc(S["log_ready"], 1)

            def stats_of(s, tile_rows, st_sem):
                for b in range(BT):
                    op = dve.bn_stats(stats[:, s, b, :], tile_rows(b))
                op.then_inc(st_sem, 1)

            def moments_of(s, st_sem, mo_sem, n):
                dve.wait_ge(st_sem, n + 1)
                dve.memset(start[:, START - 1:START], 0.0)
                for b in range(BT):
                    op = dve.bn_aggr(moments[:, s, b, :], stats[:, s, b, :])
                op.then_inc(mo_sem, 1)

            def residual_and_stats(k, s, mixed, x_count):
                dve.wait_ge(S["t_psum"], k + (CREDIT + 1))
                dve.wait_ge(x_loaded[s], x_count)
                dve.wait_ge(S["x1_kept_ready"], k + 1)
                if mixed:
                    dve.wait_ge(stored[s], mixed * (16 * pairs))
                dve.tensor_tensor(y[:, s], psum[:, T_BANK + s, :].rearrange("p (b d) -> p b d", b=BT), x_res[:, s],
                                  ALU.add).then_inc(S["y_done"], 1)
                dve.wait_ge(S["y_done"], k + 1)
                stats_of(s, lambda b: y[:, s, b, :], S["stats_done"])

            def tile_moments(k, s):
                moments_of(s, S["stats_done"], S["moments_done"], k)

            def keep(k, s, place):
                dve.wait_ge(S["x1_done"], k + 1)
                dve.tensor_copy(place, y[:, s]).then_inc(S["x1_kept_ready"], 1)

            def query_and_value_lo(k, h):
                dve.wait_ge(S["hi_ready"], 2 * k + (h + 1))
                dve.tensor_tensor(xq_lo[:, h], psum[:, QV_BANK + h, :].rearrange("p (b w) -> p b w", b=2)[:, :, 0:P],
                                  xq_hi[:, h].bitcast(F32), SUB).then_inc(S["xq_ready"], 1)
                cols = bass.ds(k * BT + 2 * h, 2)
                dve.tensor_tensor(lo_t[:, cols, :], psum[:, QV_BANK + h, :].rearrange("p (b w) -> p b w", b=2)[:, :, P:2 * P],
                                  hi_t[:, cols, :].bitcast(F32), SUB).then_inc(S["xv_ready"], 1)

            def leaky_relu(k, h):
                dve.wait_ge(S["slope_ready"], 2 * k + (h + 1))
                dve.tensor_tensor(leaky[:, h], psum[:, Z_BANK + h, :].rearrange("p (b e) -> p b e", b=2), leaky[:, h],
                                  ALU.max).then_inc(S["leaky_ready"], 1)

            def softmax(g):
                dve.wait_ge(S["row_copied"], g + 1)
                dve.tensor_tensor(rows[:, :], rows[:, :], log_row[:, :], ALU.add).then_inc(S["log_added"], 1)
                dve.wait_ge(S["log_added"], g + 1)
                dve.tensor_tensor_scan(row_a[:, :], cap_f[:, :], rows[:, :], -FLT_MAX, ALU.min, ALU.max).then_inc(S["max_f"], 1)
                dve.wait_ge(S["max_f"], g + 1)
                dve.tensor_tensor_scan(row_b[:, ::-1], cap_b[:, ::-1], row_a[:, ::-1], -FLT_MAX, ALU.min, ALU.max).then_inc(S["max_b"], 1)
                dve.wait_ge(S["max_b"], g + 1)
                dve.tensor_tensor(row_c[:, :], rows[:, :], row_b[:, :], SUB).then_inc(S["below_max"], 1)
                dve.wait_ge(S["exp_done"], g + 1)
                dve.tensor_tensor_scan(row_a[:, :], same_f[:, :], row_d[:, :], 0.0, ALU.mult, ALU.add).then_inc(S["sum_f"], 1)
                dve.wait_ge(S["sum_f"], g + 1)
                dve.tensor_tensor_scan(row_b[:, ::-1], cap_b[:, ::-1], row_a[:, ::-1], 0.0, ALU.min, ALU.max).then_inc(S["sum_b"], 1)
                dve.wait_ge(S["sum_b"], g + 1)
                dve.reciprocal(row_c[:, :], row_b[:, :]).then_inc(S["recip_done"], 1)
                dve.wait_ge(S["recip_done"], g + 1)
                dve.tensor_tensor(row_a[:, :], row_d[:, :], row_c[:, :], ALU.mult).then_inc(S["attn_row"], 1)

            def attention_out(g):
                dve.wait_ge(S["attn_psum"], g + 1)
                dve.tensor_copy(attn[:, :, :], psum[:, ATTN_BANK, 0:EC * P].rearrange("p (c r) -> p c r", c=EC)).then_inc(S["attn_ready"], 1)
                dve.wait_ge(S["attn_ready"], g + 1)

            def weight_values(k, j, s, ahead):
                dve.wait_ge(S["vg_psum"], k + 1)
                for c in range(EC):
                    w = attn[:, c, bass.ds(j * (2 * BT * HEADS) + (2 * ahead + s) * BT * HEADS, BT * HEADS)]
                    op = dve.tensor_tensor(va[:, s, c, :].rearrange("p (r d) -> p r d", d=DH),
                                           psum[:, VG_BANK + 2 * s + c, :].rearrange("p (r d) -> p r d", d=DH),
                                           w.unsqueeze(2).broadcast_to([P, BT * HEADS, DH]), ALU.mult)
                op.then_inc(S["va_ready"], 1)

            def mix_pair(g, j, last):
                if not last:
                    for s in range(2):
                        weight_values(tile_of(g, j, 2 + s), j, s, 1)
                first = [kept_from[g] * 2 * BT + s * BT for s in range(2)]
                for s in range(2):
                    k = tile_of(g, j, s)
                    place = x1_kept[:, bass.ds(j * (2 * BT) + first[s], BT), :]
                    dve.wait_ge(S["o_psum"], k + 1)
                    dve.tensor_tensor(place, psum[:, O_BANK + s, :].rearrange("p (b d) -> p b d", b=BT), place,
                                      ALU.add).then_inc(S["o_read"], 1)
                for s in range(2):
                    k = tile_of(g, j, s)
                    dve.wait_ge(S["rstd2_done"], k + (CREDIT - 1))
                    dve.wait_ge(S["o_read"], k + (CREDIT + 1))
                    dve.memset(start[:, START - 2:START - 1], 0.0)
                    stats_of(s, lambda b: x1_kept[:, bass.ds(j * (2 * BT) + (first[s] + b), 1), :].rearrange("p o d -> p (o d)"),
                             S["stats2_done"])
                    moments_of(s, S["stats2_done"], S["moments2_done"], k)

            for s in range(2):
                residual_and_stats(s, s, 0, 16)
                tile_moments(s, s)
            for s in range(2):
                keep(s, s, x1_kept[:, kept_from[0] * 2 * BT + s * BT:kept_from[0] * 2 * BT + (s + 1) * BT, :])
            mixed = 0
            for phase, g in phases:
                if phase == "edges":
                    if g > 0:
                        softmax(g - 1)
                    for j, last in steps(dve, g == groups - 1):
                        k, ahead = tile_of(g, j, 0), tile_of(g, j, 2)
                        over = isinstance(j, int)
                        if not last:
                            at = kept_from[g + 1] * 2 * BT if over else j * (2 * BT) + (kept_from[g] + 1) * 2 * BT
                        x_count = (j + 1) * 16 + (g * pairs * 16 + 16)
                        if not last:
                            residual_and_stats(ahead, 0, mixed, x_count)
                        query_and_value_lo(k, 0)
                        if not last:
                            tile_moments(ahead, 0)
                        query_and_value_lo(k, 1)
                        leaky_relu(k, 0)
                        query_and_value_lo(k + 1, 0)
                        if not last:
                            residual_and_stats(ahead + 1, 1, mixed, x_count)
                        leaky_relu(k, 1)
                        if not last:
                            tile_moments(ahead + 1, 1)
                        query_and_value_lo(k + 1, 1)
                        leaky_relu(k + 1, 0)
                        if not last:
                            keep(ahead, 0, x1_kept[:, bass.ds(at, BT), :])
                        leaky_relu(k + 1, 1)
                        if not last:
                            keep(ahead + 1, 1, x1_kept[:, bass.ds(at + BT, BT), :])
                    if g > 0:
                        attention_out(g - 1)
                    if g == groups - 1:
                        softmax(g)
                else:
                    if g == groups - 1:
                        attention_out(g)
                    for s in range(2):
                        weight_values(tile_of(g, 0, s), 0, s, 0)
                    for j, last in steps(dve, True):
                        mix_pair(g, j, last)
                    mixed += 1


def program(nc, x, adj, Wg0, bg0, Wg1, bg1, Wih, Whh, bih, bhh, W_lin, W_val, a, W_out, src, dst, out):
    B = x.shape[0]
    with ExitStack() as ctx:
        hT_hi = ctx.enter_context(nc.sbuf_tensor("hT_hi", [P, B * P], F32R))
        hT_lo = ctx.enter_context(nc.sbuf_tensor("hT_lo", [P, B * P], F32R))
        ident = ctx.enter_context(nc.sbuf_tensor("ident", [P, P], F32))
        adj_sb = ctx.enter_context(nc.sbuf_tensor("adj_sb", [P, P], F32))
        psum = ctx.enter_context(nc.psum_tensor("psum", [P, 8, BANK], F32))
        front(nc, hT_hi, hT_lo, ident, adj_sb, psum, x, adj, Wg0, bg0, Wg1, bg1, Wih, Whh, bih, bhh)
        back(nc, hT_hi, hT_lo, ident, adj_sb, psum, x, W_lin, W_val, a, W_out, src, dst, out)


_INPUTS = ("x", "adj", "L0_gnn_Wg0", "L0_gnn_bg0", "L0_gnn_Wg1", "L0_gnn_bg1", "L0_gnn_Wih", "L0_gnn_Whh", "L0_gnn_bih",
           "L0_gnn_bhh", "L1_gnn_W_lin", "L1_gnn_W_val", "L1_gnn_a", "L1_gnn_W_out", "L1_gnn_src", "L1_gnn_dst")


def kernel(**inputs):
    import numpy as np
    import concourse.bacc as bacc
    from concourse.bass_utils import run_bass_kernel_spmd

    nc = bacc.Bacc("TRN2", target_bir_lowering=False, num_devices=1)
    arrays, args = {}, []
    for name in _INPUTS:
        array = np.ascontiguousarray(inputs[name])
        arrays[name] = array
        args.append(nc.dram_tensor(name, array.shape, mybir.dt.from_np(array.dtype), kind="ExternalInput").ap())
    args.append(nc.dram_tensor("out", arrays["x"].shape, F32, kind="ExternalOutput").ap())
    program(nc, *args)
    return run_bass_kernel_spmd(nc, [arrays], core_ids=[0]).results[0]["out"]
```

```python
from contextlib import ExitStack

import concourse.bass as bass
from concourse import mybir
from concourse.alu_op_type import AluOpType as ALU

F32 = mybir.dt.float32
F32R = mybir.dt.float32r
I32 = mybir.dt.int32
ACT = mybir.ActivationFunctionType

P = 128
BANK = 512
SKIPS = 4
GATES = 4
I, F, G, O = range(GATES)
LN_EPS = 1e-5
LOG_EPS = 1e-8
SLOPE = 0.2
FLT_MAX = 3.4028234e38

BT = 4
GNN_SLOTS = 4


def loop(engine, first, end):
    return engine.bass.Fori(first, end, engines=(engine.engine,), hint_back_edge=True)


class LstmPhase:

    def __init__(self, p, batches, pairs, n_batch, items_before, f_before, tiles_before):
        self.p, self.batches, self.pairs = p, batches, pairs
        self.windows = P // p
        self.width = batches * self.windows
        self.iters = n_batch // (batches * 2 * pairs)
        self.per_iter = 2 * p * pairs
        self.f_per_iter = 2 * (p - 1) * pairs
        self.items_before, self.f_before = items_before, f_before
        self.tiles_per_iter = 2 * pairs
        self.tiles_before = tiles_before
        self.tiles_after = tiles_before + self.iters * self.tiles_per_iter
        self.items_after = items_before + self.iters * self.per_iter
        self.f_after = f_before + self.iters * self.f_per_iter

    def body(self):
        forgets = 0
        for pair in range(self.pairs):
            for t in range(self.p):
                for s in range(2):
                    forgets += t > 0
                    yield 2 * pair + s, t, 2 * (pair * self.p + t) + s, forgets


def lstm_phases(n_batch):
    phases, items, forgets, tiles = [], 0, 0, 0
    for p, batches, pairs in ((1, 4, 4), (2, 8, 2), (3, 8, 2), (4, 16, 2)):
        phases.append(LstmPhase(p, batches, pairs, n_batch, items, forgets, tiles))
        items, forgets, tiles = phases[-1].items_after, phases[-1].f_after, phases[-1].tiles_after
    return phases


def front(nc, hT_hi, hT_lo, ident, adj_sb, psum, x, adj, Wg0, bg0, Wg1, bg1, Wih, Whh, bih, bhh):
    B = x.shape[0]
    tiles = B // BT
    gnn_iters = tiles // GNN_SLOTS
    phases = lstm_phases(B)
    TW = BT * P
    DEG_LO, BIAS_LO = 32, 64
    RANKS = BIAS_LO + 1

    with ExitStack() as ctx:
        def sb(name, shape, dt=F32):
            return ctx.enter_context(nc.sbuf_tensor(name, shape, dt))

        def sem(name):
            return ctx.enter_context(nc.semaphore(name))

        adjT = sb("adjT", [P, P])
        wg0 = sb("wg0", [P, P])
        wg1_hi = sb("wg1_hi", [P, P], F32R)
        wg1_lo = sb("wg1_lo", [P, P], F32R)
        ones = sb("ones", [P, RANKS])
        start = sb("start", [P, 4])
        deg_rows = sb("deg_rows", [RANKS, BT, P], F32R)
        bg0_rows = sb("bg0_rows", [RANKS, BT, P], F32R)
        bg1_rows = sb("bg1_rows", [RANKS, P], F32R)
        w_hi = sb("w_hi", [P, SKIPS, 2, GATES, P], F32R)
        w_lo = sb("w_lo", [P, SKIPS, 2, GATES, P], F32R)
        b_raw = sb("b_raw", [SKIPS * GATES, 2, P])
        b_sum = sb("b_sum", [SKIPS * GATES, P])
        bias = sb("bias", [P, SKIPS * GATES])

        work = sb("work", [P, 15, BANK])
        axT = [work[:, s, :] for s in range(GNN_SLOTS)]
        h1 = [work[:, 4 + s, :].rearrange("p (b h) -> p b h", b=BT) for s in range(GNN_SLOTS)]
        x_tile = [work[:, 8 + s, :].rearrange("p (b d) -> p b d", b=BT) for s in range(GNN_SLOTS)]
        wg1 = work[:, 12, 0:P]
        bg0_raw = work[0:RANKS, 13, :].rearrange("p (b h) -> p b h", b=BT)
        bg1_raw = work[0:RANKS, 12, P:2 * P]
        w_raw = work[:, 0:2 * SKIPS, :].rearrange("p (r j) (g d) -> p r j g d", r=SKIPS, g=GATES)
        gate = [[work[:, 4 * s + g, :] for g in range(GATES)] for s in range(2)]
        cell = [work[:, 8 + s, :] for s in range(2)]
        in_gate = work[:, 10, :]
        tanh_c = [work[:, 11 + s, :] for s in range(2)]
        h_full = [work[:, 13 + s, :] for s in range(2)]
        hs_hi = sb("hs_hi", [P, 2, BANK], F32R)
        hs_lo = sb("hs_lo", [P, 2, BANK], F32R)

        ident_zero, ident_ready = sem("ident_zero"), sem("ident_ready")
        ones_ready = sem("ones_ready")
        adj_loaded, gnn_w_loaded, b_loaded = sem("adj_loaded"), sem("gnn_w_loaded"), sem("b_loaded")
        w_loaded = [[sem(f"w_loaded{p}_{j}") for j in range(2)] for p in range(SKIPS)]
        x_loaded = [sem(f"x_loaded{s}") for s in range(GNN_SLOTS)]
        adjT_psum, adjT_ready, deg_psum, deg_ready = (sem(n) for n in ("adjT_psum", "adjT_ready", "deg_psum", "deg_ready"))
        b_summed, b_psum, b_ready = sem("b_summed"), sem("b_psum"), sem("b_ready")
        w_psum, w_hi_ready, w_lo_ready = sem("w_psum"), sem("w_hi_ready"), sem("w_lo_ready")
        ax_psum, axT_ready = sem("ax_psum"), sem("axT_ready")
        h1_psum, h1_ready = sem("h1_psum"), sem("h1_ready")
        ah_psum, ahT_hi, ahT_ready = sem("ah_psum"), sem("ahT_hi"), sem("ahT_ready")
        bias_hi, bias_rows_ready, wg1_cut, wg1_ready = sem("bias_hi"), sem("bias_rows_ready"), sem("wg1_cut"), sem("wg1_ready")
        deg_hi = sem("deg_hi")
        h2_psum, h2_hi, h2_done = sem("h2_psum"), sem("h2_hi"), sem("h2_done")
        gate_psum = [sem(f"gate_psum_{n}") for n in "ifgo"]
        gates_read = sem("gates_read")
        f_ready, ig_ready, tanh_ready = sem("f_ready"), sem("ig_ready"), sem("tanh_ready")
        fc_done, ig_done, c_ready = sem("fc_done"), sem("ig_done"), sem("c_ready")
        h_mul, h_hi, h_done = sem("h_mul"), sem("h_hi"), sem("h_done")
        tiles_done = sem("tiles_done")
        CREDIT = 2

        hi_bt = hT_hi[:, :].rearrange("p (b t) -> p b t", t=P)
        lo_bt = hT_lo[:, :].rearrange("p (b t) -> p b t", t=P)

        def windows_at(ph, view, it, tile, t):
            first = (it * (2 * ph.pairs) + tile) * ph.batches
            return view[:, bass.ds(first, ph.batches), t:t + (ph.windows - 1) * ph.p + 1:ph.p]

        def as_windows(ph, flat):
            return flat.rearrange("p (b w) -> p b w", b=ph.batches)

        W_BANKS = 4

        def w_bank(k):
            return 4 + k % W_BANKS

        block = ctx.enter_context(nc.Block())

        @block.sync
        def _(sp):
            sp.dma_start(adj_sb[:, :], adj).then_inc(adj_loaded, 16)
            sp.dma_start(wg0[:, :], Wg0).then_inc(gnn_w_loaded, 16)
            sp.dma_start(wg1, Wg1).then_inc(gnn_w_loaded, 16)
            for b in range(BT):
                sp.dma_start(bg0_raw[:, b, :], bg0.rearrange("(a h) -> a h", a=1).broadcast_to([RANKS, P])).then_inc(gnn_w_loaded, 16)
            sp.dma_start(bg1_raw, bg1.rearrange("(a h) -> a h", a=1).broadcast_to([RANKS, P])).then_inc(gnn_w_loaded, 16)
            sp.dma_start(b_raw[:, 0, :], bih.rearrange("s (g h) -> (s g) h", g=GATES)).then_inc(b_loaded, 16)
            sp.dma_start(b_raw[:, 1, :], bhh.rearrange("s (g h) -> (s g) h", g=GATES)).then_inc(b_loaded, 16)
            for s in range(GNN_SLOTS):
                sp.dma_start(x_tile[s], x[s * BT:(s + 1) * BT].rearrange("b t d -> t b d")).then_inc(x_loaded[s], 16)
            with loop(sp, 0, gnn_iters - 1) as it:
                for s in range(GNN_SLOTS):
                    sp.wait_ge(ax_psum, it * GNN_SLOTS + s + 1)
                    src = x[bass.ds((it * GNN_SLOTS + GNN_SLOTS + s) * BT, BT)]
                    sp.dma_start(x_tile[s], src.rearrange("b t d -> t b d")).then_inc(x_loaded[s], 16)

        @block.gpsimd
        def _(pool):
            pool.memset(ident[:, :], 0.0).then_inc(ident_zero, 1)
            pool.wait_ge(ident_zero, 1)
            pool.affine_select(out=ident[:, :], in_=ident[:, :], compare_op=ALU.not_equal, fill=1.0, base=0,
                               pattern=[[-1, P]], channel_multiplier=1).then_inc(ident_ready, 1)
            for p in range(SKIPS):
                pool.dma_start(w_raw[:, p, 0], Wih[p].rearrange("(g h) d -> h g d", g=GATES)).then_inc(w_loaded[p][0], 16)
            for ph in phases:
                with loop(pool, 0, ph.iters) as it:
                    for tile, t, k, forgets in ph.body():
                        if t == ph.p - 1:
                            pool.wait_ge(h_hi, it * ph.per_iter + (ph.items_before + k + 1))
                            hi, lo = windows_at(ph, hi_bt, it, tile, t), windows_at(ph, lo_bt, it, tile, t)
                            pool.tensor_tensor(lo, as_windows(ph, h_full[k % 2][:, 0:ph.width]), hi.bitcast(F32),
                                               ALU.subtract).then_inc(tiles_done, 1)

        @block.tensor
        def _(pe):
            pe.wait_ge(adj_loaded, 16)
            pe.wait_ge(ident_ready, 1)
            pe.transpose(psum[:, 0, 0:P], adj_sb[:, :], ident[:, :]).then_inc(adjT_psum, 1)
            pe.wait_ge(adjT_ready, 1)
            pe.wait_ge(ones_ready, 1)
            pe.matmul(psum[0:RANKS, 1, 0:P], ones[:, :], adjT[:, :], start=True, stop=True).then_inc(deg_psum, 1)
            for k in range(2 * SKIPS):
                p, j = k // 2, k % 2
                pe.wait_ge(w_loaded[p][j], 16)
                if k >= W_BANKS:
                    pe.wait_ge(w_lo_ready, k - W_BANKS + 1)
                for g in range(GATES):
                    mm = pe.transpose(psum[:, w_bank(k), g * P:(g + 1) * P], w_raw[:, p, j, g, :], ident[:, :])
                mm.then_inc(w_psum, 1)

            pe.wait_ge(b_summed, 1)
            n = SKIPS * GATES
            pe.transpose(psum[:, 3, 0:n], b_sum[:, :], ident[0:n, 0:n]).then_inc(b_psum, 1)
            pe.wait_ge(gnn_w_loaded, 16 * (3 + BT))
            with loop(pe, 0, gnn_iters) as it:
                for s in range(GNN_SLOTS):
                    pe.wait_ge(x_loaded[s], it * 16 + 16)
                    if s == 2:
                        pe.wait_ge(w_lo_ready, 2 * SKIPS)
                    for b in range(BT):
                        mm = pe.matmul(psum[:, 2 * s, b * P:(b + 1) * P], x_tile[s][:, b, :], adjT[:, :], start=True, stop=True)
                    mm.then_inc(ax_psum, 1)
                pe.wait_ge(bias_rows_ready, 1)
                pe.wait_ge(b_ready, 1)
                for s in range(GNN_SLOTS):
                    out = psum[:, 2 * s + 1, :]
                    pe.wait_ge(h2_done, it * GNN_SLOTS + s + 1)
                    pe.matmul(out, deg_rows[:, 0, :], bg0_rows[:, :, :], start=True, stop=False, skip_group_check=True)
                    pe.wait_ge(axT_ready, it * GNN_SLOTS + s + 1)
                    for b in range(BT):
                        mm = pe.matmul(out[:, b * P:(b + 1) * P], axT[s][:, b * P:(b + 1) * P], wg0[:, :], start=False,
                                       stop=(b == BT - 1), skip_group_check=True)
                    mm.then_inc(h1_psum, 1)
                for s in range(GNN_SLOTS):
                    pe.wait_ge(h1_ready, it * GNN_SLOTS + s + 1)
                    for b in range(BT):
                        mm = pe.matmul(psum[:, 2 * s, b * P:(b + 1) * P], h1[s][:, b, :], adjT[:, :], start=True, stop=True)
                    mm.then_inc(ah_psum, 1)
                pe.wait_ge(wg1_ready, 1)
                for s in range(GNN_SLOTS):
                    out = psum[:, 2 * s + 1, :]
                    pe.matmul(out, bg1_rows[:, :], deg_rows[:, :, :], start=True, stop=False)
                    pe.wait_ge(ahT_ready, it * GNN_SLOTS + s + 1)
                    cols = bass.ds(it * (GNN_SLOTS * TW) + s * TW, TW)
                    pe.matmul(out, wg1_hi[:, :], hT_hi[:, cols], start=False, stop=False)
                    pe.matmul(out, wg1_hi[:, :], hT_lo[:, cols], start=False, stop=False)
                    pe.matmul(out, wg1_lo[:, :], hT_hi[:, cols], start=False, stop=True).then_inc(h2_psum, 1)

            pe.wait_ge(h2_done, tiles + GNN_SLOTS)
            for ph in phases:
                with loop(pe, 0, ph.iters) as it:
                    def from_input(tile, t, k):
                        n = it * ph.per_iter + (ph.items_before + k)
                        pe.wait_ge(gates_read, n + (CREDIT - 1))
                        if t == 0 and ph.p > 1:
                            last = phases[ph.p - 2]
                            per_tile = ph.batches // last.batches
                            pe.wait_ge(tiles_done, it * (ph.tiles_per_iter * per_tile)
                                       + (last.tiles_before + (tile + 1) * per_tile + CREDIT))
                        xh, xl = windows_at(ph, hi_bt, it, tile, t), windows_at(ph, lo_bt, it, tile, t)
                        for g in ((I, G, O) if t == 0 else (F, I, G, O)):
                            out = psum[:, 4 * (k % 2) + g, 0:ph.width]
                            wh, wl = w_hi[:, ph.p - 1, 0, g, :], w_lo[:, ph.p - 1, 0, g, :]
                            pe.matmul(out, wh, xh, start=True, stop=False)
                            pe.matmul(out, wh, xl, start=False, stop=False)
                            mm = pe.matmul(out, wl, xh, start=False, stop=(t == 0))
                            if t == 0:
                                mm.then_inc(gate_psum[g], 1)

                    def from_state(k, forgets):
                        n = it * ph.per_iter + (ph.items_before + k)
                        s = k % 2
                        hh, hl = hs_hi[:, s, 0:ph.width], hs_lo[:, s, 0:ph.width]
                        pe.wait_ge(h_hi, n - 1)
                        for g in (F, I, G, O):
                            out = psum[:, 4 * s + g, 0:ph.width]
                            wh, wl = w_hi[:, ph.p - 1, 1, g, :], w_lo[:, ph.p - 1, 1, g, :]
                            pe.matmul(out, wh, hh, start=False, stop=False)
                            pe.matmul(out, wl, hh, start=False, stop=False)
                            if g == F:
                                pe.wait_ge(h_done, it * ph.f_per_iter + (ph.f_before + forgets))
                            pe.matmul(out, wh, hl, start=False, stop=True).then_inc(gate_psum[g], 1)

                    for tile, t, k, forgets in ph.body():
                        from_input(tile, t, k)
                        if t > 0:
                            from_state(k, forgets)

        @block.scalar
        def _(act):
            for p in range(SKIPS):
                act.dma_start(w_raw[:, p, 1], Whh[p].rearrange("(g h) d -> h g d", g=GATES)).then_inc(w_loaded[p][1], 16)
            for k in range(2 * SKIPS):
                p, j = k // 2, k % 2
                act.wait_ge(w_psum, k + 1)
                act.activation(w_hi[:, p, j], psum[:, w_bank(k), :].rearrange("p (g h) -> p g h", g=GATES),
                               ACT.Copy).then_inc(w_hi_ready, 1)
            with loop(act, 0, gnn_iters) as it:
                for s in range(GNN_SLOTS):
                    act.wait_ge(ax_psum, it * GNN_SLOTS + s + 1)
                    act.activation(axT[s], psum[:, 2 * s, :], ACT.Copy).then_inc(axT_ready, 1)
                for s in range(GNN_SLOTS):
                    act.wait_ge(ah_psum, it * GNN_SLOTS + s + 1)
                    cols = bass.ds(it * (GNN_SLOTS * TW) + s * TW, TW)
                    act.activation(hT_hi[:, cols], psum[:, 2 * s, :], ACT.Copy).then_inc(ahT_hi, 1)
                for s in range(GNN_SLOTS):
                    act.wait_ge(h2_psum, it * GNN_SLOTS + s + 1)
                    cols = bass.ds((it * GNN_SLOTS + s) * TW, TW)
                    act.activation(hT_hi[:, cols], psum[:, 2 * s + 1, :], ACT.Relu).then_inc(h2_hi, 1)

            act.wait_ge(b_ready, 1)
            act.wait_ge(h1_ready, tiles)
            for ph in phases:
                with loop(act, 0, ph.iters) as it:
                    def tanh_of(k):
                        n = it * ph.per_iter + (ph.items_before + k)
                        act.wait_ge(c_ready, n + 1)
                        act.activation(tanh_c[k % 2][:, 0:ph.width], cell[k % 2][:, 0:ph.width], ACT.Tanh).then_inc(tanh_ready, 1)

                    pending = None
                    for tile, t, k, forgets in ph.body():
                        n = it * ph.per_iter + (ph.items_before + k)
                        nf = it * ph.f_per_iter + (ph.f_before + forgets)
                        s = k % 2
                        for g in ((I, G, O) if t == 0 else (F, I, G, O)):
                            act.wait_ge(gate_psum[g], nf if g == F else n + 1)
                            if g == O:
                                act.wait_ge(h_mul, n + (CREDIT - 1))
                            b = (ph.p - 1) * GATES + g
                            op = act.activation(gate[s][g][:, 0:ph.width], psum[:, 4 * s + g, 0:ph.width],
                                                ACT.Tanh if g == G else ACT.Sigmoid, bias=bias[:, b:b + 1])
                            if g == F:
                                op.then_inc(f_ready, 1)
                            elif g == G:
                                op.then_inc(ig_ready, 1)
                            elif g == O:
                                op.then_inc(gates_read, 1)
                            if pending is not None:
                                tanh_of(pending)
                                pending = None
                        if k + 1 < ph.per_iter and (k + 1) % (2 * ph.p) < 2:
                            pending = k
                        else:
                            tanh_of(k)

        @block.vector
        def _(dve):
            dve.memset(ones[:, :], 1.0).then_inc(ones_ready, 1)
            dve.memset(bg0_rows[:, :, :].bitcast(F32), 0.0)
            dve.memset(bg1_rows[:, :].bitcast(F32), 0.0).then_inc(ones_ready, 1)
            dve.wait_ge(ones_ready, 2)
            dve.memset(start[:, 0:1], 0.0).then_inc(h2_done, GNN_SLOTS)
            dve.memset(start[:, 1:2], 0.0).then_inc(gates_read, CREDIT)
            dve.memset(start[:, 2:3], 0.0).then_inc(tiles_done, CREDIT)
            dve.memset(start[:, 3:4], 0.0).then_inc(h_mul, CREDIT)
            dve.wait_ge(adjT_psum, 1)
            dve.tensor_copy(adjT[:, :], psum[:, 0, 0:P]).then_inc(adjT_ready, 1)
            dve.wait_ge(deg_psum, 1)
            for b in range(BT):
                op = dve.tensor_copy(deg_rows[:, b, :], psum[0:RANKS, 1, 0:P])
            op.then_inc(deg_hi, 1)
            dve.wait_ge(deg_hi, 1)
            lo = slice(DEG_LO, DEG_LO + 1)
            for b in range(BT):
                op = dve.tensor_tensor(deg_rows[lo, b, :], psum[lo, 1, 0:P], deg_rows[lo, b, :].bitcast(F32), ALU.subtract)
            op.then_inc(deg_ready, 1)
            for k in range(2 * SKIPS):
                p, j = k // 2, k % 2
                if k == W_BANKS:
                    dve.wait_ge(b_loaded, 32)
                    dve.tensor_tensor(b_sum[:, :], b_raw[:, 0, :], b_raw[:, 1, :], ALU.add).then_inc(b_summed, 1)
                dve.wait_ge(w_hi_ready, k + 1)
                dve.tensor_tensor(w_lo[:, p, j], psum[:, w_bank(k), :].rearrange("p (g h) -> p g h", g=GATES),
                                  w_hi[:, p, j].bitcast(F32), ALU.subtract).then_inc(w_lo_ready, 1)
            dve.wait_ge(b_psum, 1)
            dve.tensor_copy(bias[:, :], psum[:, 3, 0:SKIPS * GATES]).then_inc(b_ready, 1)
            dve.wait_ge(gnn_w_loaded, 16 * (3 + BT))
            for rows, raw in ((bg0_rows, bg0_raw), (bg1_rows, bg1_raw)):
                for at in (0, DEG_LO, BIAS_LO):
                    op = dve.tensor_copy(rows[at:at + 1], raw[at:at + 1])
            op.then_inc(bias_hi, 1)
            dve.wait_ge(bias_hi, 1)
            lo = slice(BIAS_LO, BIAS_LO + 1)
            for rows, raw in ((bg0_rows, bg0_raw), (bg1_rows, bg1_raw)):
                op = dve.tensor_tensor(rows[lo], raw[lo], rows[lo].bitcast(F32), ALU.subtract)
            op.then_inc(bias_rows_ready, 1)
            dve.tensor_copy(wg1_hi[:, :], wg1).then_inc(wg1_cut, 1)
            dve.wait_ge(wg1_cut, 1)
            dve.tensor_tensor(wg1_lo[:, :], wg1, wg1_hi[:, :].bitcast(F32), ALU.subtract).then_inc(wg1_ready, 1)
            with loop(dve, 0, gnn_iters) as it:
                for s in range(GNN_SLOTS):
                    dve.wait_ge(h1_psum, it * GNN_SLOTS + s + 1)
                    dve.tensor_scalar(h1[s], psum[:, 2 * s + 1, :].rearrange("p (b h) -> p b h", b=BT), 0.0, None,
                                      ALU.max).then_inc(h1_ready, 1)
                for s in range(GNN_SLOTS):
                    dve.wait_ge(ahT_hi, it * GNN_SLOTS + s + 1)
                    cols = bass.ds(it * (GNN_SLOTS * TW) + s * TW, TW)
                    dve.tensor_tensor(hT_lo[:, cols], psum[:, 2 * s, :], hT_hi[:, cols].bitcast(F32),
                                      ALU.subtract).then_inc(ahT_ready, 1)
                for s in range(GNN_SLOTS):
                    dve.wait_ge(h2_hi, it * GNN_SLOTS + s + 1)
                    cols = bass.ds(it * (GNN_SLOTS * TW) + s * TW, TW)
                    dve.scalar_tensor_tensor(out=hT_lo[:, cols], in0=psum[:, 2 * s + 1, :], scalar=0.0,
                                             in1=hT_hi[:, cols].bitcast(F32), op0=ALU.max,
                                             op1=ALU.subtract).then_inc(h2_done, 1)

            for ph in phases:
                with loop(dve, 0, ph.iters) as it:
                    def place(tile, t, k):
                        if t == ph.p - 1:
                            return (windows_at(ph, hi_bt, it, tile, t), windows_at(ph, lo_bt, it, tile, t),
                                    as_windows(ph, h_full[k % 2][:, 0:ph.width]))
                        return hs_hi[:, k % 2, 0:ph.width], hs_lo[:, k % 2, 0:ph.width], h_full[k % 2][:, 0:ph.width]

                    def split(tile, t, k, forgets):
                        n = it * ph.per_iter + (ph.items_before + k)
                        hi, lo, full = place(tile, t, k)
                        dve.wait_ge(h_mul, n + (CREDIT + 1))
                        dve.tensor_copy(hi, full).then_inc(h_hi, 1)
                        if t < ph.p - 1:
                            dve.wait_ge(h_hi, n + 1)
                            dve.tensor_tensor(lo, full, hi.bitcast(F32), ALU.subtract).then_inc(h_done, 1)

                    before = None
                    for tile, t, k, forgets in ph.body():
                        n = it * ph.per_iter + (ph.items_before + k)
                        nf = it * ph.f_per_iter + (ph.f_before + forgets)
                        s = k % 2
                        c = cell[s][:, 0:ph.width]
                        if t > 0:
                            dve.wait_ge(f_ready, nf)
                            dve.tensor_tensor(c, c, gate[s][F][:, 0:ph.width], ALU.mult).then_inc(fc_done, 1)
                        dve.wait_ge(ig_ready, n + 1)
                        i_g = c if t == 0 else in_gate[:, 0:ph.width]
                        op = dve.tensor_tensor(i_g, gate[s][I][:, 0:ph.width], gate[s][G][:, 0:ph.width], ALU.mult)
                        if t == 0:
                            op.then_inc(c_ready, 1)
                        else:
                            op.then_inc(ig_done, 1)
                            dve.wait_ge(fc_done, nf)
                            dve.wait_ge(ig_done, nf)
                            dve.tensor_tensor(c, c, i_g, ALU.add).then_inc(c_ready, 1)
                        if before:
                            split(*before)
                            before = None
                        dve.wait_ge(tanh_ready, n + 1)
                        if t == 0:
                            dve.wait_ge(tiles_done, it * ph.tiles_per_iter + (ph.tiles_before + tile - 1 + CREDIT))
                        dve.tensor_tensor(h_full[s][:, 0:ph.width], gate[s][O][:, 0:ph.width], tanh_c[s][:, 0:ph.width],
                                          ALU.mult).then_inc(h_mul, 1)
                        if t == ph.p - 1:
                            before = (tile, t, k, forgets)
                        else:
                            split(tile, t, k, forgets)
                    if before:
                        split(*before)


def back(nc, hT_hi, hT_lo, ident, adj_sb, psum, x, W_lin, W_val, a, W_out, src, dst, out):
    B = x.shape[0]
    tiles = B // BT
    TW = BT * P
    HEADS, DH = a.shape
    E = src.shape[0]
    EC = E // P
    GROUP = P // HEADS
    groups = B // GROUP
    pairs = GROUP // BT // 2
    GT = 2 * pairs
    KEPT = 2 * pairs + 1
    kept_from = [(1 + g * pairs) % KEPT for g in range(groups)]
    assert all(first + pairs <= KEPT for first in kept_from)
    phases = [("edges", 0)]
    for g in range(1, groups):
        phases += [("edges", g), ("mix", g - 1)]
    phases += [("mix", groups - 1)]

    with ExitStack() as ctx:
        def sb(name, shape, dt=F32):
            return ctx.enter_context(nc.sbuf_tensor(name, shape, dt))

        def sem(name):
            return ctx.enter_context(nc.semaphore(name))

        x1_kept = sb("x1_kept", [P, KEPT * 2 * BT, P])
        room = sb("room", [P, 2 * EC * TW + 2 * TW])
        space, taken = [x1_kept[:, :, :].rearrange("p b d -> p (b d)")], [3 * 2 * TW]

        def part(width):
            taken[0] += width
            return space[0][:, taken[0] - width:taken[0]]

        edge_row_i = part(2 * E).bitcast(I32).rearrange("p (j e) -> p j e", j=2)
        edge_col_i = sb("edge_col_i", [P, 2, EC], I32)
        edge_row = part(2 * E).rearrange("p (j e) -> p j e", j=2)
        edge_col = sb("edge_col", [P, EC, 2])
        count_i = part(E).bitcast(I32)
        count = part(E)
        index_i = sb("index_i", [P, EC], I32)
        index = sb("index", [P, EC])
        key_row = part(E)
        key_col = sb("key_col", [P, EC])
        less = part(E)
        rank = sb("rank", [P, EC])
        permute = part(EC * E).rearrange("p (c e) -> p c e", c=EC)
        spread = part(2 * EC * P).rearrange("p (j c n) -> p j c n", j=2, c=EC)
        sorted_row = part(2 * E).rearrange("p (j e) -> p j e", j=2)
        sorted_col = sb("sorted_col", [P, EC, 2])
        at_node = part(2 * E).rearrange("p (j e) -> p j e", j=2)
        to_r = sb("to_r", [P, E], F32R)
        ends = sb("ends", [P, E], F32R)
        from_node = sb("from_node", [P, EC, P])
        to_node = part(EC * P).rearrange("p (c n) -> p c n", c=EC)
        adj_edge = sb("adj_edge", [P, EC])
        log_adj = sb("log_adj", [P, EC])
        log_row = sb("log_row", [P, E])
        same_f, same_b = sb("same_f", [P, E]), part(E)
        cap_f, cap_b = sb("cap_f", [P, E]), sb("cap_b", [P, E])
        ones = sb("ones2", [P, P])
        minus_half = sb("minus_half", [P, BT])
        eps = sb("eps", [P, BT])
        zero = sb("zero", [P, BT])
        START = 12
        start = sb("start2", [P, START])
        w_nat = part(3 * P).rearrange("p (j d) -> p j d", j=3)
        w_qv = sb("w_qv", [P, 2 * P])
        w_outT = sb("w_outT", [P, P])
        PAIR_ROWS = 2 * BT * HEADS
        A_COL = PAIR_ROWS - HEADS
        a_wide = sb("a_wide", [P, A_COL + P])

        space[0], taken[0] = room, 0
        hsum = part(2 * TW).rearrange("p (s b t) -> p s b t", s=2, b=BT)
        leaky = part(4 * E).rearrange("p (h b e) -> p h b e", h=2, b=2)
        row_bcd = part(3 * E).rearrange("p (n e) -> p n e", n=3)
        xq_hi = sb("xq_hi", [P, 2, 2, P], F32R)
        xq_lo = sb("xq_lo", [P, 2, 2, P], F32R)
        x_res = sb("x_res", [P, 2, BT, P])
        y = sb("y", [P, 2, BT, P])
        stats = sb("stats", [P, 2, BT, 6])
        SECOND = 2
        moments = sb("moments", [P, 4, BT, 2])
        var_eps = sb("var_eps", [P, 4, BT])
        rstd = sb("rstd", [P, 4, BT])
        minus_mean = sb("minus_mean", [P, 4, BT])
        shift = sb("shift", [P, 4, BT])
        taken[0] = 0
        va = part(2 * EC * TW).rearrange("p (s c w) -> p s c w", s=2, c=EC)
        yT = part(2 * TW).rearrange("p (s w) -> p s w", s=2)
        x1T = sb("x1T", [P, 2, TW])
        row_a = sb("row_a", [P, E])
        attn = sb("attn", [P, EC, P])
        log_diag = attn
        rows = sb("rows", [P, E])

        names = ("ones_done rows_loaded cols_loaded w_loaded a_loaded iota_done a_zero tables_f ranks permutes spreads rows_psum "
                 "rows_ready onehots adj_psum adj_done eps_done log_done diag_done log_psum log_ready ends_ready sames shifted caps wT_psum wT_ready "
                 "key_done ecol_done "
                 "hsum_ready t_psum y_done stats_done moments_done var_done rstd_done shift_done x1_done x1_kept_ready xt_psum xT_ready "
                 "qv_psum xq_ready hi_ready xv_ready z_psum slope_ready leaky_ready edges_psum "
                 "row_copied log_added max_f max_b below_max exp_done sum_f sum_b recip_done attn_row attn_psum attn_ready "
                 "vg_psum va_ready yt_psum yT_ready o_psum o_read stats2_done moments2_done var2_done rstd2_done shift2_done out_ready")
        S = {n: sem("b_" + n) for n in names.split()}
        x_loaded = [sem(f"b_x_loaded{s}") for s in range(2)]
        stored = [sem(f"b_stored{s}") for s in range(2)]
        CREDIT = 2

        T_BANK, QV_BANK, Z_BANK, SCORE_BANK = 0, 2, 4, 6
        VG_BANK, YT_BANK, O_BANK = 0, 4, 6
        ATTN_BANK = Z_BANK
        SUB = ALU.subtract

        block = ctx.enter_context(nc.Block())

        hi_t = hT_hi[:, :].rearrange("p (b d) -> p b d", d=P)
        lo_t = hT_lo[:, :].rearrange("p (b d) -> p b d", d=P)

        def softmax_rows(g):
            held = x1T[:, :, :].rearrange("p s w -> p (s w)")[:, 0:3 * E].rearrange("p (n e) -> p n e", n=3) if g == groups - 1 else row_bcd
            return held[:, 0, :], held[:, 1, :], held[:, 2, :]

        score_banks = psum[:, SCORE_BANK:SCORE_BANK + 2, :].rearrange("p k c -> p (k c)")

        def tile_of(g, j, s):
            return g * GT + s + 2 * j

        def steps(engine, last):
            with loop(engine, 0, pairs - 1) as j:
                yield j, False
            yield pairs - 1, last

        @block.sync
        def _(sp):
            for s in range(2):
                sp.dma_start(x_res[:, s], x[s * BT:(s + 1) * BT].rearrange("b t d -> t b d")).then_inc(x_loaded[s], 16)
            for j, e in enumerate((src, dst)):
                sp.dma_start(edge_row_i[:, j, :], e.rearrange("(a e) -> a e", a=1).broadcast_to([P, E])).then_inc(S["rows_loaded"], 16)
            for j, w in enumerate((W_lin, W_val, W_out)):
                sp.dma_start(w_nat[:, j, :], w).then_inc(S["w_loaded"], 16)
            with loop(sp, 0, tiles // 2 - 1) as it:
                for s in range(2):
                    sp.wait_ge(S["y_done"], 2 * it + s + 1)
                    sp.dma_start(x_res[:, s], x[bass.ds((2 * it + 2 + s) * BT, BT)].rearrange("b t d -> t b d")).then_inc(x_loaded[s], 16)

        @block.gpsimd
        def _(pool):
            pool.memset(a_wide[:, :], 0.0).then_inc(S["a_zero"], 1)
            pool.iota(count_i[:, :], pattern=[[1, E]], base=0, channel_multiplier=0).then_inc(S["iota_done"], 1)
            pool.iota(index_i[:, :], pattern=[[P, EC]], base=0, channel_multiplier=1).then_inc(S["iota_done"], 1)

            def norm_factors(s, ready, var_sem, rstd_sem, shift_sem, k, credit=0):
                pool.wait_ge(ready, k + 1)
                if credit:
                    pool.wait_ge(S["out_ready"], k + (credit - 1))
                pool.tensor_tensor(var_eps[:, s, :], moments[:, s, :, 1], eps[:, :], ALU.add).then_inc(var_sem, 1)
                pool.tensor_tensor(minus_mean[:, s, :], zero[:, :], moments[:, s, :, 0], SUB)
                pool.wait_ge(var_sem, k + 1)
                pool.tensor_tensor(rstd[:, s, :], var_eps[:, s, :], minus_half[:, :], ALU.pow).then_inc(rstd_sem, 1)
                pool.wait_ge(rstd_sem, k + (credit + 1))
                pool.tensor_tensor(shift[:, s, :], minus_mean[:, s, :], rstd[:, s, :], ALU.mult).then_inc(shift_sem, 1)

            def sum_parts(k):
                for s in range(2):
                    pool.wait_ge(S["t_psum"], k + s + 1)
                    cols = bass.ds((k + s) * TW, TW)
                    pool.tensor_tensor(hsum[:, s].rearrange("p b t -> p (b t)"), hT_hi[:, cols].bitcast(F32),
                                       hT_lo[:, cols].bitcast(F32), ALU.add).then_inc(S["hsum_ready"], 1)

            def factors(k):
                for s in range(2):
                    norm_factors(s, S["moments_done"], S["var_done"], S["rstd_done"], S["shift_done"], k + s)

            def mix_factors(g, j):
                for s in range(2):
                    norm_factors(SECOND + s, S["moments2_done"], S["var2_done"], S["rstd2_done"], S["shift2_done"], tile_of(g, j, s), CREDIT)

            sum_parts(0)
            factors(0)
            for phase, g in phases:
                if phase == "edges":
                    ahead_pairs = pairs - (g == groups - 1)
                    if g >= 2:
                        factors(tile_of(g, 0, 2))
                    with loop(pool, 0 if g < 2 else 1, ahead_pairs) as j:
                        sum_parts(tile_of(g, j, 2))
                        factors(tile_of(g, j, 2))
                else:
                    with loop(pool, 0, pairs - 1) as j:
                        mix_factors(g, j)
                    if g < groups - 2:
                        pool.wait_ge(S["yt_psum"], (g + 1) * GT)
                        sum_parts(tile_of(g + 2, 0, 2))
                    mix_factors(g, pairs - 1)

        @block.tensor
        def _(pe):
            def turn_h(k, s):
                pe.wait_ge(S["hsum_ready"], k + 1)
                for b in range(BT):
                    mm = pe.transpose(psum[:, T_BANK + s, b * P:(b + 1) * P], hsum[:, s, b, :], ident[:, :])
                mm.then_inc(S["t_psum"], 1)

            def turn_x1(k, s):
                pe.wait_ge(S["x1_done"], k + 1)
                for b in range(BT):
                    mm = pe.transpose(psum[:, T_BANK + s, b * P:(b + 1) * P], y[:, s, b, :], ident[:, :])
                mm.then_inc(S["xt_psum"], 1)

            for s in range(2):
                turn_h(s, s)
            pe.wait_ge(S["permutes"], EC)
            pe.wait_ge(S["spreads"], 2 * EC)
            for j in range(2):
                for c in range(EC):
                    pe.matmul(psum[:, 2, j * E:(j + 1) * E], spread[:, j, c, :], permute[:, c, :], start=(c == 0), stop=(c == EC - 1))
            for r in range(EC):
                for c in range(EC):
                    mm = pe.matmul(psum[:, 3, 2 * r:2 * r + 2], permute[:, c, r * P:(r + 1) * P], edge_col[:, c, :],
                                   start=(c == 0), stop=(c == EC - 1))
            mm.then_inc(S["rows_psum"], 1)
            pe.wait_ge(S["w_loaded"], 48)
            for j in range(3):
                mm = pe.transpose(psum[:, 6, j * P:(j + 1) * P], w_nat[:, j, :], ident[:, :])
            mm.then_inc(S["wT_psum"], 1)
            pe.wait_ge(S["onehots"], 2)
            for c in range(EC):
                mm = pe.matmul(psum[:, 4, c * P:(c + 1) * P], at_node[:, 0, c * P:(c + 1) * P], adj_sb[:, :], start=True, stop=True)
            mm.then_inc(S["adj_psum"], 1)
            for s in range(2):
                turn_x1(s, s)
            pe.wait_ge(S["wT_ready"], 2)
            pe.wait_ge(S["ends_ready"], 1)
            pe.wait_ge(S["a_loaded"], 16 * HEADS)

            def project(k, s, h):
                pe.wait_ge(S["xT_ready"], k + 1)
                pe.wait_ge(S["xv_ready"], 2 * k + (h + 1))
                for b in range(2):
                    mm = pe.matmul(psum[:, QV_BANK + h, b * 2 * P:(b + 1) * 2 * P], x1T[:, s, (2 * h + b) * P:(2 * h + b + 1) * P],
                                   w_qv[:, :], start=True, stop=True)
                mm.then_inc(S["qv_psum"], 1)

            def gather(k, h):
                pe.wait_ge(S["xq_ready"], 2 * k + (h + 1))
                for b in range(2):
                    z = psum[:, Z_BANK + h, b * E:(b + 1) * E]
                    pe.matmul(z, xq_hi[:, h, b, :], ends[:, :], start=True, stop=False)
                    mm = pe.matmul(z, xq_lo[:, h, b, :], ends[:, :], start=False, stop=True)
                mm.then_inc(S["z_psum"], 1)

            def edge_scores(g, k, j, s, h):
                pe.wait_ge(S["leaky_ready"], 2 * k + (h + 1))
                if s == 0 and h == 0 and g > 0:
                    pe.wait_ge(S["row_copied"], g)
                for b in range(2):
                    n = s * BT + 2 * h + b
                    mm = pe.matmul(score_banks[:, bass.ds(j * E, E)], a_wide[:, A_COL - n * HEADS:A_COL - n * HEADS + P],
                                   leaky[:, h, b, :], start=(n == 0), stop=(n == 2 * BT - 1), skip_group_check=True)
                return mm

            def edge_pair(g, j, last):
                k, ahead = tile_of(g, j, 0), tile_of(g, j, 2)
                pe.wait_ge(S["xT_ready"], k + 1)
                if not last:
                    turn_h(ahead, 0)
                project(k, 0, 0)
                project(k, 0, 1)
                if not last:
                    pe.wait_ge(S["xT_ready"], k + 2)
                    turn_h(ahead + 1, 1)
                gather(k, 0)
                project(k + 1, 1, 0)
                gather(k, 1)
                project(k + 1, 1, 1)
                edge_scores(g, k, j, 0, 0)
                gather(k + 1, 0)
                edge_scores(g, k, j, 0, 1)
                gather(k + 1, 1)
                edge_scores(g, k + 1, j, 1, 0)
                if not last:
                    turn_x1(ahead, 0)
                edge_scores(g, k + 1, j, 1, 1).then_inc(S["edges_psum"], 1)
                if not last:
                    turn_x1(ahead + 1, 1)

            def attention_by_edge(g):
                pe.wait_ge(S["attn_row"], g + 1)
                for c in range(EC):
                    mm = pe.transpose(psum[:, ATTN_BANK, c * P:(c + 1) * P], row_a[:, c * P:(c + 1) * P], ident[:, :])
                mm.then_inc(S["attn_psum"], 1)

            def value_gather(k, j, s):
                for c in range(EC):
                    out_c = psum[:, VG_BANK + 2 * s + c, :]
                    to = to_r[:, c * P:(c + 1) * P]
                    pe.matmul(out_c, to, hi_t[:, bass.ds(k * BT, BT), :], start=True, stop=False)
                    mm = pe.matmul(out_c, to, lo_t[:, bass.ds(k * BT, BT), :], start=False, stop=True)
                mm.then_inc(S["vg_psum"], 1)

            def sum_by_source(k, s):
                pe.wait_ge(S["va_ready"], k + 1)
                for b in range(BT):
                    for c in range(EC):
                        mm = pe.matmul(psum[:, YT_BANK + s, b * P:(b + 1) * P], va[:, s, c, b * P:(b + 1) * P],
                                       from_node[:, c, :], start=(c == 0), stop=(c == EC - 1))
                mm.then_inc(S["yt_psum"], 1)

            def output(k, s):
                pe.wait_ge(S["yT_ready"], k + 1)
                pe.wait_ge(S["o_read"], k + 1)
                for b in range(BT):
                    mm = pe.matmul(psum[:, O_BANK + s, b * P:(b + 1) * P], yT[:, s, b * P:(b + 1) * P], w_outT[:, :],
                                   start=True, stop=True)
                mm.then_inc(S["o_psum"], 1)

            def mix_pair(g, j, last):
                k = tile_of(g, j, 0)
                for s in range(2):
                    sum_by_source(k + s, s)
                if not last:
                    for s in range(2):
                        value_gather(tile_of(g, j, 2 + s), j, s)
                for s in range(2):
                    output(k + s, s)

            mixed = 0
            for phase, g in phases:
                if phase == "edges":
                    pe.wait_ge(S["o_read"], mixed * GT + CREDIT)
                    for j, last in steps(pe, g == groups - 1):
                        edge_pair(g, j, last)
                    if g == 0:
                        pe.wait_ge(S["diag_done"], EC)
                        for c in range(EC):
                            mm = pe.matmul(psum[:, ATTN_BANK, c * P:(c + 1) * P], ones[:, :], log_diag[:, c, :], start=True, stop=True)
                        mm.then_inc(S["log_psum"], 1)
                    if g > 0:
                        attention_by_edge(g - 1)
                        pe.wait_ge(S["attn_ready"], g)
                else:
                    if g == groups - 1:
                        attention_by_edge(g)
                    started = min(g + 2, groups)
                    pe.wait_ge(S["xT_ready"], min(started * GT + 2, tiles))
                    pe.wait_ge(S["xv_ready"], 2 * started * GT + CREDIT)
                    pe.wait_ge(S["row_copied"], started)
                    for s in range(2):
                        value_gather(tile_of(g, 0, s), 0, s)
                    for j, last in steps(pe, True):
                        mix_pair(g, j, last)
                    mixed += 1

        @block.scalar
        def _(act):
            for j, e in enumerate((src, dst)):
                act.dma_start(edge_col_i[:, j, :], e.rearrange("(c p) -> p c", p=P), allow_slow_non_contiguous=True).then_inc(S["cols_loaded"], 16)
            act.wait_ge(S["a_zero"], 1)
            for h in range(HEADS):
                act.dma_start(a_wide[h * DH:(h + 1) * DH, A_COL + h:A_COL + h + 1], a[h].rearrange("(d o) -> d o", o=1),
                              allow_slow_non_contiguous=True).then_inc(S["a_loaded"], 16)

            def half_bank(h):
                return psum[:, QV_BANK + h, :].rearrange("p (b w) -> p b w", b=2)

            def query_and_value(k, h):
                act.wait_ge(S["qv_psum"], 2 * k + (h + 1))
                act.activation(xq_hi[:, h], half_bank(h)[:, :, 0:P], ACT.Copy)
                act.activation(hi_t[:, bass.ds(k * BT + 2 * h, 2), :], half_bank(h)[:, :, P:2 * P], ACT.Copy).then_inc(S["hi_ready"], 1)

            def slope_times(k, h):
                act.wait_ge(S["z_psum"], 2 * k + (h + 1))
                act.activation(leaky[:, h], psum[:, Z_BANK + h, :].rearrange("p (b e) -> p b e", b=2), ACT.Copy,
                               scale=SLOPE).then_inc(S["slope_ready"], 1)

            def normalize(slot, row_of, shift_sem, done_sem, n):
                act.wait_ge(shift_sem, n + 1)
                for b in range(BT):
                    op = act.activation(row_of(b), row_of(b), ACT.Identity, bias=shift[:, slot, b:b + 1], scale=rstd[:, slot, b:b + 1])
                op.then_inc(done_sem, 1)

            def normalize_x1(k, s):
                normalize(s, lambda b: y[:, s, b, :], S["shift_done"], S["x1_done"], k)

            def x1_turned(k, s):
                act.wait_ge(S["xt_psum"], k + 1)
                act.activation(x1T[:, s, :], psum[:, T_BANK + s, :], ACT.Copy).then_inc(S["xT_ready"], 1)

            def exponentials(g):
                _, below, exps = softmax_rows(g)
                act.wait_ge(S["below_max"], g + 1)
                act.activation(exps, below, ACT.Exp).then_inc(S["exp_done"], 1)

            def copy_yT(g, j):
                for s in range(2):
                    act.wait_ge(S["yt_psum"], tile_of(g, j, s) + 1)
                    act.activation(yT[:, s, :], psum[:, YT_BANK + s, :], ACT.Copy).then_inc(S["yT_ready"], 1)

            def normalize_and_store(g, j):
                for s in range(2):
                    k = tile_of(g, j, s)
                    first = kept_from[g] * 2 * BT + s * BT
                    normalize(SECOND + s, lambda b: x1_kept[:, bass.ds(j * (2 * BT) + (first + b), 1), :].rearrange("p o d -> p (o d)"),
                              S["shift2_done"], S["out_ready"], k)
                for s in range(2):
                    k = tile_of(g, j, s)
                    first = kept_from[g] * 2 * BT + s * BT
                    act.wait_ge(S["out_ready"], k + (CREDIT + 1))
                    act.dma_start(out[bass.ds(k * BT, BT)].rearrange("b t d -> t b d"),
                                  x1_kept[:, bass.ds(j * (2 * BT) + first, BT), :]).then_inc(stored[s], 16)

            def edge_pair(g, j, last, mixed_before=None, softmax_of=-1):
                k = tile_of(g, j, 0)
                query_and_value(k, 0)
                query_and_value(k, 1)
                slope_times(k, 0)
                query_and_value(k + 1, 0)
                if softmax_of >= 0:
                    exponentials(softmax_of)
                slope_times(k, 1)
                if mixed_before is not None:
                    normalize_and_store(mixed_before, pairs - 1)
                query_and_value(k + 1, 1)
                slope_times(k + 1, 0)
                if not last:
                    normalize_x1(tile_of(g, j, 2), 0)
                slope_times(k + 1, 1)
                if not last:
                    normalize_x1(tile_of(g, j, 3), 1)
                    for s in range(2):
                        x1_turned(tile_of(g, j, 2 + s), s)

            for s in range(2):
                normalize_x1(s, s)
            act.wait_ge(S["eps_done"], 1)
            act.activation(log_adj[:, :], adj_edge[:, :], ACT.Ln).then_inc(S["log_done"], 1)
            for s in range(2):
                x1_turned(s, s)
            for phase, g in phases:
                if phase == "edges":
                    if g >= 2:
                        edge_pair(g, 0, False, g - 2)
                        with loop(act, 1, pairs - 1) as j:
                            edge_pair(g, j, False)
                    else:
                        with loop(act, 0, pairs - 1) as j:
                            edge_pair(g, j, False)
                    edge_pair(g, pairs - 1, g == groups - 1, None, g - 1)
                    act.wait_ge(S["edges_psum"], (g + 1) * pairs)
                    for j in range(pairs):
                        op = act.activation(rows[j * PAIR_ROWS:(j + 1) * PAIR_ROWS, :], score_banks[0:PAIR_ROWS, j * E:(j + 1) * E], ACT.Copy)
                    op.then_inc(S["row_copied"], 1)
                else:
                    if g == groups - 2:
                        exponentials(g + 1)
                    copy_yT(g, 0)
                    with loop(act, 0, pairs - 1) as j:
                        copy_yT(g, j + 1)
                        normalize_and_store(g, j)
                    if g >= groups - 2:
                        normalize_and_store(g, pairs - 1)
            for s in range(2):
                act.wait_ge(stored[s], 16 * (tiles // 2))

        @block.vector
        def _(dve):
            dve.memset(ones[:, :], 1.0).then_inc(S["ones_done"], 1)
            dve.memset(minus_half[:, :], -0.5).then_inc(S["ones_done"], 1)
            dve.memset(eps[:, :], LN_EPS).then_inc(S["ones_done"], 1)
            dve.memset(zero[:, :], 0.0).then_inc(S["ones_done"], 1)
            for n, freed in enumerate((S["t_psum"], S["x1_kept_ready"], S["xv_ready"], S["o_read"], S["out_ready"], S["rstd2_done"])):
                dve.memset(start[:, n:n + 1], 0.0).then_inc(freed, CREDIT)

            def stats_of(s, tile_rows, st_sem):
                for b in range(BT):
                    op = dve.bn_stats(stats[:, s, b, :], tile_rows(b))
                op.then_inc(st_sem, 1)

            def moments_of(s, slot, st_sem, mo_sem, n):
                dve.wait_ge(st_sem, n + 1)
                dve.memset(start[:, START - 1:START], 0.0)
                for b in range(BT):
                    op = dve.bn_aggr(moments[:, slot, b, :], stats[:, s, b, :])
                op.then_inc(mo_sem, 1)

            def residual(k, s, x_count):
                dve.wait_ge(S["t_psum"], k + (CREDIT + 1))
                dve.wait_ge(x_loaded[s], x_count)
                dve.wait_ge(S["x1_kept_ready"], k + 1)
                dve.tensor_tensor(y[:, s], psum[:, T_BANK + s, :].rearrange("p (b d) -> p b d", b=BT), x_res[:, s],
                                  ALU.add).then_inc(S["y_done"], 1)

            def tile_stats(k, s):
                dve.wait_ge(S["y_done"], k + 1)
                stats_of(s, lambda b: y[:, s, b, :], S["stats_done"])

            def tile_moments(k, s):
                moments_of(s, s, S["stats_done"], S["moments_done"], k)

            def keep(k, s, place, mixed=0):
                if mixed:
                    dve.wait_ge(stored[s], mixed * (16 * pairs))
                dve.wait_ge(S["x1_done"], k + 1)
                dve.tensor_copy(place, y[:, s]).then_inc(S["x1_kept_ready"], 1)

            dve.wait_ge(S["rows_loaded"], 32)
            dve.tensor_copy(edge_row, edge_row_i).then_inc(S["tables_f"], 1)
            dve.wait_ge(S["cols_loaded"], 32)
            for j in range(2):
                dve.tensor_copy(edge_col[:, :, j], edge_col_i[:, j, :]).then_inc(S["ecol_done"], 1)
            dve.wait_ge(S["iota_done"], 2)
            dve.tensor_copy(count[:, :], count_i[:, :]).then_inc(S["tables_f"], 1)
            dve.tensor_copy(index[:, :], index_i[:, :]).then_inc(S["tables_f"], 1)
            dve.wait_ge(S["tables_f"], 3)
            dve.wait_ge(S["ecol_done"], 2)
            dve.scalar_tensor_tensor(out=key_row[:, :], in0=edge_row[:, 0, :], scalar=float(E), in1=count[:, :],
                                     op0=ALU.mult, op1=ALU.add).then_inc(S["key_done"], 1)
            dve.scalar_tensor_tensor(out=key_col[:, :], in0=edge_col[:, :, 0], scalar=float(E), in1=index[:, :],
                                     op0=ALU.mult, op1=ALU.add).then_inc(S["key_done"], 1)
            for c in range(EC):
                for j in range(2):
                    dve.tensor_scalar(spread[:, j, c, :], ones[:, :], edge_col[:, c, j:j + 1], None, ALU.mult).then_inc(S["spreads"], 1)
            dve.wait_ge(S["key_done"], 2)
            for c in range(EC):
                if c:
                    dve.wait_ge(S["ranks"], c)
                dve.tensor_scalar(less[:, :], key_row[:, :], key_col[:, c:c + 1], 0.0, ALU.is_lt, ALU.add,
                                  accum_out=rank[:, c:c + 1]).then_inc(S["ranks"], 1)
            dve.wait_ge(S["ranks"], EC)
            for c in range(EC):
                dve.tensor_scalar(permute[:, c, :], count[:, :], rank[:, c:c + 1], None, ALU.is_equal).then_inc(S["permutes"], 1)
            for s in range(2):
                residual(s, s, 16)
                tile_stats(s, s)
                tile_moments(s, s)

            dve.wait_ge(S["wT_psum"], 1)
            dve.tensor_copy(w_qv[:, :], psum[:, 6, 0:2 * P]).then_inc(S["wT_ready"], 1)
            dve.tensor_copy(w_outT[:, :], psum[:, 6, 2 * P:3 * P]).then_inc(S["wT_ready"], 1)
            dve.wait_ge(S["rows_psum"], 1)
            dve.tensor_copy(sorted_row, psum[:, 2, :].rearrange("p (j e) -> p j e", j=2)).then_inc(S["rows_ready"], 1)
            dve.tensor_copy(sorted_col[:, :, :], psum[:, 3, 0:2 * EC].rearrange("p (c j) -> p c j", j=2)).then_inc(S["rows_ready"], 1)
            dve.memset(same_f[:, 0:1], 0.0)
            dve.memset(same_b[:, E - 1:E], 0.0).then_inc(S["rows_ready"], 1)
            dve.wait_ge(S["rows_ready"], 3)
            for j in range(2):
                dve.tensor_scalar(at_node[:, j, :], sorted_row[:, j, :], index[:, 0:1], None, ALU.is_equal).then_inc(S["onehots"], 1)
            for j, of_edge in enumerate((from_node, to_node)):
                for c in range(EC):
                    op = dve.tensor_scalar(of_edge[:, c, :], count[:, 0:P], sorted_col[:, c, j:j + 1], None, ALU.is_equal)
            op.then_inc(S["onehots"], 1)
            dve.wait_ge(S["onehots"], 3)
            dve.tensor_copy(to_r[:, :], at_node[:, 1, :])
            dve.tensor_tensor(ends[:, :], at_node[:, 0, :], at_node[:, 1, :], ALU.add).then_inc(S["ends_ready"], 1)
            dve.tensor_tensor(same_f[:, 1:E], sorted_row[:, 0, 1:E], sorted_row[:, 0, 0:E - 1], ALU.is_equal)
            dve.tensor_tensor(same_b[:, 0:E - 1], sorted_row[:, 0, 1:E], sorted_row[:, 0, 0:E - 1], ALU.is_equal).then_inc(S["sames"], 1)
            dve.wait_ge(S["sames"], 1)
            for same, cap in ((same_f, row_a), (same_b, rows)):
                dve.tensor_scalar(cap[:, :], same[:, :], 2.0, -1.0, ALU.mult, ALU.add).then_inc(S["shifted"], 1)
            dve.wait_ge(S["shifted"], 2)
            for sign, cap in ((row_a, cap_f), (rows, cap_b)):
                dve.tensor_scalar(cap[:, :], sign[:, :], FLT_MAX, None, ALU.mult).then_inc(S["caps"], 1)
            for s in range(2):
                keep(s, s, x1_kept[:, kept_from[0] * 2 * BT + s * BT:kept_from[0] * 2 * BT + (s + 1) * BT, :])
            dve.wait_ge(S["adj_psum"], 1)
            for c in range(EC):
                if c:
                    dve.wait_ge(S["adj_done"], c)
                dve.tensor_tensor_reduce(less[:, 0:P], psum[:, 4, c * P:(c + 1) * P], to_node[:, c, :], 1.0, 0.0,
                                         ALU.mult, ALU.add, rank[:, c:c + 1]).then_inc(S["adj_done"], 1)
            dve.wait_ge(S["adj_done"], EC)
            dve.tensor_scalar(adj_edge[:, :], rank[:, :], LOG_EPS, None, ALU.add).then_inc(S["eps_done"], 1)
            dve.wait_ge(S["log_done"], 1)
            for c in range(EC):
                dve.tensor_scalar(log_diag[:, c, :], ident[:, :], log_adj[:, c:c + 1], None, ALU.mult).then_inc(S["diag_done"], 1)

            def query_and_value_lo(k, h):
                dve.wait_ge(S["hi_ready"], 2 * k + (h + 1))
                dve.tensor_tensor(xq_lo[:, h], psum[:, QV_BANK + h, :].rearrange("p (b w) -> p b w", b=2)[:, :, 0:P],
                                  xq_hi[:, h].bitcast(F32), SUB).then_inc(S["xq_ready"], 1)
                cols = bass.ds(k * BT + 2 * h, 2)
                dve.tensor_tensor(lo_t[:, cols, :], psum[:, QV_BANK + h, :].rearrange("p (b w) -> p b w", b=2)[:, :, P:2 * P],
                                  hi_t[:, cols, :].bitcast(F32), SUB).then_inc(S["xv_ready"], 1)

            def leaky_relu(k, h):
                dve.wait_ge(S["slope_ready"], 2 * k + (h + 1))
                dve.tensor_tensor(leaky[:, h], psum[:, Z_BANK + h, :].rearrange("p (b e) -> p b e", b=2), leaky[:, h],
                                  ALU.max).then_inc(S["leaky_ready"], 1)

            SOFTMAX_STEPS = 8

            def softmax(g, step):
                backwards, below, exps = softmax_rows(g)
                if step == 0:
                    dve.wait_ge(S["row_copied"], g + 1)
                    dve.tensor_tensor(rows[:, :], rows[:, :], log_row[:, :], ALU.add).then_inc(S["log_added"], 1)
                elif step == 1:
                    dve.wait_ge(S["log_added"], g + 1)
                    dve.tensor_tensor_scan(row_a[:, :], cap_f[:, :], rows[:, :], -FLT_MAX, ALU.min, ALU.max).then_inc(S["max_f"], 1)
                elif step == 2:
                    dve.wait_ge(S["max_f"], g + 1)
                    dve.tensor_tensor_scan(backwards[:, ::-1], cap_b[:, ::-1], row_a[:, ::-1], -FLT_MAX, ALU.min, ALU.max).then_inc(S["max_b"], 1)
                elif step == 3:
                    dve.wait_ge(S["max_b"], g + 1)
                    dve.tensor_tensor(below, rows[:, :], backwards, SUB).then_inc(S["below_max"], 1)
                elif step == 4:
                    dve.wait_ge(S["exp_done"], g + 1)
                    dve.tensor_tensor_scan(row_a[:, :], same_f[:, :], exps, 0.0, ALU.mult, ALU.add).then_inc(S["sum_f"], 1)
                elif step == 5:
                    dve.wait_ge(S["sum_f"], g + 1)
                    dve.tensor_tensor_scan(backwards[:, ::-1], cap_b[:, ::-1], row_a[:, ::-1], 0.0, ALU.min, ALU.max).then_inc(S["sum_b"], 1)
                elif step == 6:
                    dve.wait_ge(S["sum_b"], g + 1)
                    dve.reciprocal(below, backwards).then_inc(S["recip_done"], 1)
                else:
                    dve.wait_ge(S["recip_done"], g + 1)
                    dve.tensor_tensor(row_a[:, :], exps, below, ALU.mult).then_inc(S["attn_row"], 1)

            def attention_out(g):
                dve.wait_ge(S["attn_psum"], g + 1)
                dve.tensor_copy(attn[:, :, :], psum[:, ATTN_BANK, 0:EC * P].rearrange("p (c r) -> p c r", c=EC)).then_inc(S["attn_ready"], 1)
                dve.wait_ge(S["attn_ready"], g + 1)

            def weight_values(k, j, s, ahead):
                dve.wait_ge(S["vg_psum"], k + 1)
                for c in range(EC):
                    w = attn[:, c, bass.ds(j * (2 * BT * HEADS) + (2 * ahead + s) * BT * HEADS, BT * HEADS)]
                    op = dve.tensor_tensor(va[:, s, c, :].rearrange("p (r d) -> p r d", d=DH),
                                           psum[:, VG_BANK + 2 * s + c, :].rearrange("p (r d) -> p r d", d=DH),
                                           w.unsqueeze(2).broadcast_to([P, BT * HEADS, DH]), ALU.mult)
                op.then_inc(S["va_ready"], 1)

            def mix_pair(g, j, last):
                if not last:
                    for s in range(2):
                        weight_values(tile_of(g, j, 2 + s), j, s, 1)
                elif g == groups - 2:
                    for step in range(4, SOFTMAX_STEPS):
                        softmax(g + 1, step)
                first = [kept_from[g] * 2 * BT + s * BT for s in range(2)]
                for s in range(2):
                    k = tile_of(g, j, s)
                    place = x1_kept[:, bass.ds(j * (2 * BT) + first[s], BT), :]
                    dve.wait_ge(S["o_psum"], k + 1)
                    dve.tensor_tensor(place, psum[:, O_BANK + s, :].rearrange("p (b d) -> p b d", b=BT), place,
                                      ALU.add).then_inc(S["o_read"], 1)
                if last and g == groups - 2:
                    attention_out(g + 1)
                for s in range(2):
                    k = tile_of(g, j, s)
                    dve.wait_ge(S["rstd2_done"], k + (CREDIT - 1))
                    dve.wait_ge(S["o_read"], k + (CREDIT + 1))
                    dve.memset(start[:, START - 2:START - 1], 0.0)
                    stats_of(s, lambda b: x1_kept[:, bass.ds(j * (2 * BT) + (first[s] + b), 1), :].rearrange("p o d -> p (o d)"),
                             S["stats2_done"])
                    moments_of(s, SECOND + s, S["stats2_done"], S["moments2_done"], k)

            mixed = 0
            for phase, g in phases:
                if phase == "edges":
                    if g == 1:
                        dve.wait_ge(S["log_psum"], 1)
                        dve.tensor_copy(log_row[:, :], psum[:, ATTN_BANK, 0:E]).then_inc(S["log_ready"], 1)
                        dve.wait_ge(S["log_ready"], 1)
                    for j, last in steps(dve, g == groups - 1):
                        k, ahead = tile_of(g, j, 0), tile_of(g, j, 2)
                        over = isinstance(j, int)
                        if not last:
                            at = kept_from[g + 1] * 2 * BT if over else j * (2 * BT) + (kept_from[g] + 1) * 2 * BT
                        x_count = (j + 1) * 16 + (g * pairs * 16 + 16)

                        def before(*of_steps):
                            if over and g > 0:
                                for step in of_steps:
                                    softmax(g - 1, step)

                        if not last:
                            residual(ahead, 0, x_count)
                            tile_stats(ahead, 0)
                        query_and_value_lo(k, 0)
                        before(0)
                        if not last:
                            tile_moments(ahead, 0)
                        query_and_value_lo(k, 1)
                        before(1)
                        if not last:
                            residual(ahead + 1, 1, x_count)
                        leaky_relu(k, 0)
                        before(2)
                        query_and_value_lo(k + 1, 0)
                        before(3)
                        if not last:
                            tile_stats(ahead + 1, 1)
                        leaky_relu(k, 1)
                        before(4)
                        if not last:
                            tile_moments(ahead + 1, 1)
                        query_and_value_lo(k + 1, 1)
                        before(5)
                        leaky_relu(k + 1, 0)
                        if not last:
                            keep(ahead, 0, x1_kept[:, bass.ds(at, BT), :], mixed)
                        leaky_relu(k + 1, 1)
                        if not last:
                            keep(ahead + 1, 1, x1_kept[:, bass.ds(at + BT, BT), :], mixed)
                        before(6, 7)
                    if g > 0:
                        attention_out(g - 1)
                    if g == groups - 1:
                        for step in range(4):
                            softmax(g, step)
                else:
                    for s in range(2):
                        weight_values(tile_of(g, 0, s), 0, s, 0)
                    for j, last in steps(dve, True):
                        mix_pair(g, j, last)
                    mixed += 1


def program(nc, x, adj, Wg0, bg0, Wg1, bg1, Wih, Whh, bih, bhh, W_lin, W_val, a, W_out, src, dst, out):
    B = x.shape[0]
    with ExitStack() as ctx:
        hT_hi = ctx.enter_context(nc.sbuf_tensor("hT_hi", [P, B * P], F32R))
        hT_lo = ctx.enter_context(nc.sbuf_tensor("hT_lo", [P, B * P], F32R))
        ident = ctx.enter_context(nc.sbuf_tensor("ident", [P, P], F32))
        adj_sb = ctx.enter_context(nc.sbuf_tensor("adj_sb", [P, P], F32))
        psum = ctx.enter_context(nc.psum_tensor("psum", [P, 8, BANK], F32))
        front(nc, hT_hi, hT_lo, ident, adj_sb, psum, x, adj, Wg0, bg0, Wg1, bg1, Wih, Whh, bih, bhh)
        back(nc, hT_hi, hT_lo, ident, adj_sb, psum, x, W_lin, W_val, a, W_out, src, dst, out)


_INPUTS = ("x", "adj", "L0_gnn_Wg0", "L0_gnn_bg0", "L0_gnn_Wg1", "L0_gnn_bg1", "L0_gnn_Wih", "L0_gnn_Whh", "L0_gnn_bih",
           "L0_gnn_bhh", "L1_gnn_W_lin", "L1_gnn_W_val", "L1_gnn_a", "L1_gnn_W_out", "L1_gnn_src", "L1_gnn_dst")


def kernel(**inputs):
    import numpy as np
    import concourse.bacc as bacc
    from concourse.bass_utils import run_bass_kernel_spmd

    nc = bacc.Bacc("TRN2", target_bir_lowering=False, num_devices=1)
    arrays, args = {}, []
    for name in _INPUTS:
        array = np.ascontiguousarray(inputs[name])
        arrays[name] = array
        args.append(nc.dram_tensor(name, array.shape, mybir.dt.from_np(array.dtype), kind="ExternalInput").ap())
    args.append(nc.dram_tensor("out", arrays["x"].shape, F32, kind="ExternalOutput").ap())
    program(nc, *args)
    return run_bass_kernel_spmd(nc, [arrays], core_ids=[0]).results[0]["out"]
```
